# Optimizing a Trainium2 kernel written in Bass

```python
import numpy as np
import jax
import jax.numpy as jnp

def _softmax(x, axis=-1):
    return jax.nn.softmax(x, axis=axis)

def _gelu(x):
    return jax.nn.gelu(x, approximate=True)

def _silu(x):
    return jax.nn.silu(x)

def _sigmoid(x):
    return jax.nn.sigmoid(x)

def _layernorm(x, axis=-1, eps=1e-05):
    m = jnp.mean(x, axis=axis, keepdims=True)
    v = jnp.var(x, axis=axis, keepdims=True)
    return (x - m) / jnp.sqrt(v + eps)

def _scatter_add(tgt, idx, src, axis=0):
    return tgt.at[idx].add(src)

def _segment_sum(src, seg, n):
    return jax.ops.segment_sum(src, seg, n)
kernel_name = 'mk_flamingo_gated_d1_seqx_r8_694716'

def setup_inputs(seed: int=0):
    np.random.seed(seed)
    _w = jnp.asarray

    def _rec_inputs():
        import jax
        import jax.numpy as jnp
        _rk = jax.random.key(seed)
        x = -0.0002928 + 1 * jax.random.normal(jax.random.fold_in(_rk, 1), (16, 128, 256), jnp.float32)
        _lenS = 128 - jax.random.randint(jax.random.fold_in(_rk, 7), (16,), 0, max(1, 128 // 4) + 1, jnp.int32)
        _lenS2 = 128 - jax.random.randint(jax.random.fold_in(_rk, 8), (16,), 0, max(1, 128 // 4) + 1, jnp.int32)
        fside_S2_0 = -0.00337071 + 1.01897 * jax.random.normal(jax.random.fold_in(_rk, 11), (128,), jnp.float32)
        _ctx_2048P = jax.random.normal(jax.random.fold_in(_rk, 12), (16, 16, 256), jnp.float32)
        _ctx_2048c = jax.random.dirichlet(jax.random.fold_in(_rk, 512), 0.3 * jnp.ones((16,), jnp.float32), (16, 128))
        _ctx_2048t = jnp.einsum('bsk,bkd->bsd', _ctx_2048c, _ctx_2048P)
        _ctx_2048t = _ctx_2048t * jax.lax.rsqrt(jnp.mean(jnp.square(_ctx_2048t)) + 1e-12) * 0.953939
        ctx_2048 = 0.000675642 + 1.00031 * (_ctx_2048t + 0.3 * jax.random.normal(jax.random.fold_in(_rk, 612), (16, 128, 256), jnp.float32))
        _g = jax.random.normal(jax.random.fold_in(_rk, 9001), (2, 1), jnp.float32)
        _g = jnp.sign(_g) * jnp.maximum(jnp.abs(_g), 1.0) + (_g == 0) * 1.0
        g_xattn = _g[0]
        g_ffn = _g[1]
        return (x, fside_S2_0, ctx_2048, g_xattn, g_ffn)
    x, fside_S2_0, ctx_2048, g_xattn, g_ffn = _rec_inputs()

    def _L0_xattn_setup():
        import jax, jax.numpy as jnp
        import numpy as np
        key = jax.random.key(seed)
        ks = jax.random.split(key, 5)
        B, D, L, NH = (2, 128, 256, 8)
        H = D // NH
        return {'v': jax.random.normal(ks[0], (B, D, L), jnp.float32), 'k': jax.random.normal(ks[1], (H, L), jnp.float32) * 0.1, 'bias': jax.random.normal(ks[2], (D,), jnp.float32), 'x1': jax.random.normal(ks[3], (B, D, L), jnp.float32), 'x2': jax.random.normal(ks[4], (B, D, L), jnp.float32), 'num_heads': NH}
    _L0_xattn_all = _L0_xattn_setup()
    _L0_xattn_in = {k: v for k, v in _L0_xattn_all.items() if k in ('k',)}
    del _L0_xattn_all

    def _L0_ffn_setup():
        import jax, jax.numpy as jnp
        import numpy as np
        HIDDEN = 256
        INTER = 704
        B, S = (2, 256)

        def _ternary(key, shape):
            return jax.random.randint(key, shape, -1, 2).astype(jnp.float32)
        key = jax.random.key(seed)
        ks = jax.random.split(key, 7)
        x = jax.random.normal(ks[0], (B, S, HIDDEN), dtype=jnp.float32)
        gate_w = _ternary(ks[1], (INTER, HIDDEN))
        up_w = _ternary(ks[2], (INTER, HIDDEN))
        down_w = _ternary(ks[3], (HIDDEN, INTER))
        gate_s = jax.random.uniform(ks[4], (INTER,), minval=0.01, maxval=0.1, dtype=jnp.float32)
        up_s = jax.random.uniform(ks[5], (INTER,), minval=0.01, maxval=0.1, dtype=jnp.float32)
        down_s = jax.random.uniform(ks[6], (HIDDEN,), minval=0.01, maxval=0.1, dtype=jnp.float32)
        return {'x': x, 'gate_w': gate_w, 'up_w': up_w, 'down_w': down_w, 'gate_s': gate_s, 'up_s': up_s, 'down_s': down_s}
    _L0_ffn_all = _L0_ffn_setup()
    _L0_ffn_in = {k: v for k, v in _L0_ffn_all.items() if k in ('gate_w', 'up_w', 'down_w', 'gate_s', 'up_s', 'down_s')}
    del _L0_ffn_all
    return {'x': x, 'fside_S2_0': fside_S2_0, 'ctx_2048': ctx_2048, 'g_xattn': g_xattn, 'g_ffn': g_ffn, 'L0_xattn_k': _L0_xattn_in['k'], 'L0_ffn_gate_w': _L0_ffn_in['gate_w'], 'L0_ffn_up_w': _L0_ffn_in['up_w'], 'L0_ffn_down_w': _L0_ffn_in['down_w'], 'L0_ffn_gate_s': _L0_ffn_in['gate_s'], 'L0_ffn_up_s': _L0_ffn_in['up_s'], 'L0_ffn_down_s': _L0_ffn_in['down_s']}

def reference(x, fside_S2_0, ctx_2048, g_xattn, g_ffn, L0_xattn_k, L0_ffn_gate_w, L0_ffn_up_w, L0_ffn_down_w, L0_ffn_gate_s, L0_ffn_up_s, L0_ffn_down_s):
    import jax
    import jax.numpy as jnp

    def _L0_xattn_ref(v, k, bias, x1, x2, num_heads):
        import jax, jax.numpy as jnp
        import numpy as np
        B, D, L = v.shape
        H = D // num_heads
        fft_size = 2 * L
        vr = v.reshape(B, H, num_heads, L)
        x1r = x1.reshape(B, H, num_heads, L)
        x2r = x2.reshape(B, H, num_heads, L)
        kv = vr[:, :, :, None, :] * x2r[:, :, None, :, :]
        k_f = jnp.fft.rfft(k.astype(jnp.float32), n=fft_size)
        y = jnp.fft.irfft(jnp.fft.rfft(kv, n=fft_size) * k_f[None, :, None, None, :], n=fft_size)[..., :L]
        skip = bias.astype(jnp.float32).reshape(H, num_heads)[None, :, :, None, None]
        y = y + kv * skip
        out = jnp.einsum('bhijl,bhil->bhjl', y, x1r)
        return out.reshape(B, D, L)

    def _L0_ffn_ref(x, gate_w, up_w, down_w, gate_s, up_s, down_s):
        import jax, jax.numpy as jnp
        import numpy as np
        HIDDEN = 256
        INTER = 704
        B, S = (2, 256)

        def _ternary(key, shape):
            return jax.random.randint(key, shape, -1, 2).astype(jnp.float32)
        b, s, h = x.shape
        xf = x.reshape(b * s, h)
        g = jnp.einsum('th,ih->ti', xf, gate_w) * gate_s
        u = jnp.einsum('th,ih->ti', xf, up_w) * up_s
        hdn = jax.nn.silu(g) * u
        out = jnp.einsum('ti,hi->th', hdn, down_w) * down_s
        return out.reshape(b, s, -1)
    x = x + jnp.tanh(g_xattn[0]) * _L0_xattn_ref(_layernorm(x, axis=-1), L0_xattn_k, fside_S2_0, ctx_2048, ctx_2048, 8)
    x = x + jnp.tanh(g_ffn[0]) * _L0_ffn_ref(_layernorm(x, axis=-1), L0_ffn_gate_w, L0_ffn_up_w, L0_ffn_down_w, L0_ffn_gate_s, L0_ffn_up_s, L0_ffn_down_s)
    return x

_drawn_inputs = setup_inputs


def setup_inputs(seed=0):
    import zlib

    import numpy as np

    out = dict(_drawn_inputs(seed))
    spreads = {}
    factors = {}
    for name, (base, spread) in spreads.items():
        noise = np.random.default_rng([zlib.crc32(name.encode()), seed]).standard_normal(out[name].shape)
        drawn = base * np.exp(spread * noise) if base else spread * noise
        out[name] = jnp.asarray(drawn.astype(out[name].dtype))
    for name, factor in factors.items():
        out[name] = (out[name] * factor).astype(out[name].dtype)
    return out
```

```python
from contextlib import ExitStack

import concourse.bass as bass
from concourse import mybir

B, D, L = 16, 128, 256
NH = 8
H = D // NH
INTER = 704
P = 128
MB = L // P
EPS = 1e-5

PAIRS = NH * B * NH
BANK = 512
KC = L // P
FULL = INTER // P
REST = INTER - FULL * P
NU = FULL + 1
GU = 2 * INTER
TOK = 2 * P
SLOTS = 4
PACK = 4 * L + 4
BIAS = 4 * L

PAD = 2

GX, GF, GS, US = 0, 1, 2, 2 + NU
SCAL = 2 + 2 * NU

F32 = mybir.dt.float32
F32R = mybir.dt.float32r
ALU = mybir.AluOpType
ACT = mybir.ActivationFunctionType


def count(i, k, per=1, done=0):
    return i * (SLOTS * per) + (k * per + done)


def units(i, pair, done):
    return i * (2 * NU) + (pair // 2 * NU + done)


def has(i, k):
    return not isinstance(i, int) or 0 <= SLOTS * i + k < H


def need(eng, sem, value):
    if not isinstance(value, int) or value > 0:
        eng.wait_ge(sem, value)


def flamingo(nc, packed, scalars, gate_up_w, down_w, down_s, out):
    with ExitStack() as ctx:
        def sb(name, shape, dt=F32):
            return ctx.enter_context(nc.sbuf_tensor(name, shape, dt))

        def sem(name):
            return ctx.enter_context(nc.semaphore(name))

        ins = sb("ins", [P, SLOTS, PACK])
        xs = sb("xs", [P, SLOTS, L])
        x1 = sb("x1", [P, SLOTS, L])
        stats = sb("stats", [P, 2, 6])
        mv = sb("mv", [P, 2, 2])
        var_eps = sb("var_eps", [P, 2, 1])
        rstd = sb("rstd", [P, 2, 1])
        minus_half = sb("minus_half", [P, 1])
        v = sb("v", [P, 2, L])
        vb = sb("vb", [P, 2, L])
        vbc = sb("vbc", [P, 2, L])
        skip = sb("skip", [P, 2, L])
        vT = sb("vT", [P, 2, MB * P])
        kv = sb("kv", [P, MB, PAIRS])
        kv_hi = sb("kv_hi", [P, 2, MB, PAIRS], F32R)
        kv_lo = sb("kv_lo", [P, 2, MB, PAIRS], F32R)
        T_hi = sb("T_hi", [P, 2, L], F32R)
        T_lo = sb("T_lo", [P, 2, L], F32R)
        z = sb("z", [P, MB, PAIRS])
        xn = sb("xn", [P, 2, L])
        xT_hi = sb("xT_hi", [P, KC, TOK], F32R)
        xT_lo = sb("xT_lo", [P, KC, TOK], F32R)
        gate = sb("gate", [P, 2, TOK])
        h = sb("h", [P, 2, TOK])
        h_hi = sb("h_hi", [P, NU, TOK], F32R)
        h_lo = sb("h_lo", [P, NU, TOK], F32R)
        res = sb("res", [P, 2, L])
        scal = sb("scal", [P, SCAL])
        tanh_g = sb("tanh_g", [P, 2])
        wgu = sb("wgu", [P, KC, GU])
        wgu_hi = sb("wgu_hi", [P, KC, GU], F32R)
        wgu_lo = sb("wgu_lo", [P, KC, GU], F32R)
        wd = sb("wd", [P, NU, L])
        wd_s = sb("wd_s", [P, L])
        wd_hi = sb("wd_hi", [P, NU, L], F32R)
        wd_lo = sb("wd_lo", [P, NU, L], F32R)
        ident = sb("ident", [P, P])
        same_b = sb("same_b", [P, P])

        conv = ctx.enter_context(nc.psum_tensor("conv", [P, MB, PAIRS], F32))
        gate_ps = ctx.enter_context(nc.psum_tensor("gate_ps", [P, BANK], F32))
        up_ps = ctx.enter_context(nc.psum_tensor("up_ps", [P, BANK], F32))
        turn_ps = ctx.enter_context(nc.psum_tensor("turn_ps", [P, BANK], F32))
        out_ps = ctx.enter_context(nc.psum_tensor("out_ps", [P, BANK], F32))

        in_loaded = [sem(f"in_loaded{s}") for s in range(SLOTS)]
        scal_loaded, wgu_loaded, wd_loaded = sem("scal_loaded"), sem("wgu_loaded"), sem("wd_loaded")
        ident_ready, same_b_ready, const_step = sem("ident_ready"), sem("same_b_ready"), sem("const_step")
        tanh_ready, zero_ready = sem("tanh_ready"), sem("zero_ready")
        wgu_hi_ready, wgu_lo_ready = sem("wgu_hi_ready"), sem("wgu_lo_ready")
        wd_s_ready, wd_scaled, wd_hi_ready, wd_lo_ready = (
            sem("wd_s_ready"), sem("wd_scaled"), sem("wd_hi_ready"), sem("wd_lo_ready"))
        ln1_step, ln1_ready, half_ready = sem("ln1_step"), sem("ln1_ready"), sem("half_ready")
        v_ready, vb_ready, vbc_ready = sem("v_ready"), sem("vb_ready"), sem("vbc_ready")
        vT_done, vT_ready = sem("vT_done"), sem("vT_ready")
        skip_done, skip_ready, xs_ready = sem("skip_done"), sem("skip_ready"), sem("xs_ready")
        kv_ready, kv_hi_ready, kv_lo_ready = sem("kv_ready"), sem("kv_hi_ready"), sem("kv_lo_ready")
        T_hi_ready, T_lo_ready = sem("T_hi_ready"), sem("T_lo_ready")
        conv_done, z_ready, mix_done, x1_ready = (
            sem("conv_done"), sem("z_ready"), sem("mix_done"), sem("x1_ready"))
        ln2_step, ln2_ready = sem("ln2_step"), sem("ln2_ready")
        xn_ready, xT_done, xT_hi_ready, xT_lo_ready = (
            sem("xn_ready"), sem("xT_done"), sem("xT_hi_ready"), sem("xT_lo_ready"))
        gate_done, up_done, silu_ready = sem("gate_done"), sem("up_done"), sem("silu_ready")
        h_ready, h_hi_ready, h_lo_ready, h_rest_ready = (
            sem("h_ready"), sem("h_hi_ready"), sem("h_lo_ready"), sem("h_rest_ready"))
        down_done, res_ready = sem("down_done"), sem("res_ready")
        res_free = [sem(f"res_free{s}") for s in range(2)]

        def x_row(k):
            return ins[:, k % SLOTS, 0:L]

        def c_row(k):
            return ins[:, k % SLOTS, L:2 * L]

        def c_T(k, m):
            return ins[:, k % SLOTS, 2 * L + m * P:2 * L + (m + 1) * P]

        def T(k):
            return ins[:, k % SLOTS, 3 * L:4 * L]

        def bias(k):
            return ins[:, k % SLOTS, BIAS:BIAS + 1]

        def over_j(a):
            return a.rearrange("p (b i) -> p i b", i=NH).unsqueeze(3).broadcast_to([P, NH, B, NH])

        def over_i(a):
            return a.unsqueeze(1).broadcast_to([P, NH, P])

        def by_i(a):
            return a.rearrange("p (i n) -> p i n", i=NH)

        def by_ibj(a):
            return a.rearrange("p (i b j) -> p i b j", i=NH, b=B)

        def steps(run):
            for k in range(-2, 2):
                run(0, k)
            with nc.Fori(0, (H - 4) // SLOTS, engines=[run.engine]) as i:
                for k in range(2, 2 + SLOTS):
                    run(i, k)
            for k in range(H - 2, H + 2):
                run(0, k)

        block = ctx.enter_context(nc.Block())

        @block.sync
        def _(sp):
            def load(i, k):
                if not has(i, k):
                    return
                row = (i * SLOTS + k) * P
                need(sp, x1_ready, count(i, k - SLOTS, 1, 1))
                sp.dma_start(ins[:, k % SLOTS, :], packed[bass.ds(row, P), :]
                             ).then_inc(in_loaded[k % SLOTS], 16)

            def store(i, k):
                for s in range(2):
                    row = (i * SLOTS + k - 3 + s) * P
                    sp.wait_ge(res_ready, count(i, k - 3 + s, 1, 1))
                    sp.dma_start(out[bass.ds(row, P), :], res[:, s, :]
                                 ).then_inc(res_free[s], 16)

            def run(i, k):
                if k == -2:
                    load(i, 0)
                    sp.dma_start(scal[:, :], scalars).then_inc(scal_loaded, 16)
                    load(i, 1)
                    sp.dma_start(wgu[:, :, :], gate_up_w).then_inc(wgu_loaded, 16)
                    load(i, 2)
                    sp.wait_ge(zero_ready, 1)
                    sp.dma_start(wd[:, 0:FULL, :], down_w[0:FULL * P, :].rearrange("(c p) n -> p c n", p=P)
                                 ).then_inc(wd_loaded, 16)
                    sp.dma_start(wd[P - REST:P, FULL, :], down_w[FULL * P:INTER, :]).then_inc(wd_loaded, 16)
                    sp.dma_start(wd_s[:, :], down_s).then_inc(wd_loaded, 16)
                if k == 0:
                    load(i, 3)
                elif k > 0 and k % 2 == 0:
                    load(i, k + 2)
                    load(i, k + 3)
                if k % 2 == 1 and k >= 3:
                    store(i, k)

            run.engine = mybir.EngineType.SP
            steps(run)
            for s in range(2):
                sp.wait_ge(res_free[s], 16 * (H // 2 + 1))

        @block.gpsimd
        def _(pool):
            nc.gpsimd.memset(minus_half[:, :], -0.5).then_inc(half_ready, 1)
            nc.gpsimd.memset(ident[:, :], 0.0).then_inc(const_step, 1)
            nc.gpsimd.memset(same_b[:, :], 1.0).then_inc(const_step, 1)
            pool.wait_ge(const_step, 2)
            nc.gpsimd.affine_select(out=ident[:, :], in_=ident[:, :], compare_op=ALU.not_equal, fill=1.0, base=0,
                                    pattern=[[-1, P]], channel_multiplier=1).then_inc(ident_ready, 1)
            sb3 = same_b[:, :].rearrange("p (b j) -> p b j", j=NH)
            nc.gpsimd.affine_select(out=sb3, in_=sb3, compare_op=ALU.is_ge, fill=0.0, base=0,
                                    pattern=[[-NH, B], [0, NH]], channel_multiplier=1).then_inc(const_step, 1)
            pool.wait_ge(const_step, 3)
            nc.gpsimd.affine_select(out=sb3, in_=sb3, compare_op=ALU.is_ge, fill=0.0, base=NH - 1,
                                    pattern=[[NH, B], [0, NH]], channel_multiplier=-1).then_inc(same_b_ready, 1)

            def inverse_std(i, k, which, step, ready):
                if not has(i, k):
                    return
                if isinstance(i, int) and k == 0:
                    pool.wait_ge(half_ready, 1)
                pool.wait_ge(step, count(i, k, 3, 3))
                nc.gpsimd.tensor_tensor(rstd[:, which, :], var_eps[:, which, :], minus_half[:, :], ALU.pow
                                        ).then_inc(ready, 1)

            def products(i, k, m):
                if not has(i, k):
                    return
                if m == 0:
                    pool.wait_ge(vT_ready, count(i, k, 1, 1))
                need(pool, kv_lo_ready, count(i, k - 1, MB, m + 1))
                nc.gpsimd.tensor_tensor(by_ibj(kv[:, m, :]), over_j(vT[:, k % 2, m * P:(m + 1) * P]),
                                        c_T(k, m).rearrange("p (b j) -> p b j", j=NH).unsqueeze(1)
                                        .broadcast_to([P, NH, B, NH]), ALU.mult).then_inc(kv_ready, 1)

            def split_T(i, k):
                if not has(i, k):
                    return
                pool.wait_ge(T_hi_ready, count(i, k, 1, 1))
                nc.gpsimd.tensor_tensor(T_lo[:, k % 2, :], T(k), T_hi[:, k % 2, :].bitcast(F32),
                                        ALU.subtract).then_inc(T_lo_ready, 1)

            def skip_terms(i, k):
                if not has(i, k):
                    return
                pool.wait_ge(vb_ready, count(i, k, 1, 1))
                need(pool, skip_done, count(i, k - 2, 1, 1))
                nc.gpsimd.tensor_tensor(vbc[:, k % 2, :], vb[:, k % 2, :], c_row(k), ALU.mult
                                        ).then_inc(vbc_ready, 1)

            def add_skip(i, k):
                if not has(i, k):
                    return
                pool.wait_ge(skip_ready, count(i, k, 1, 1))
                need(pool, x1_ready, count(i, k - SLOTS, 1, 1))
                nc.gpsimd.tensor_tensor(xs[:, k % SLOTS, :], x_row(k), skip[:, k % 2, :], ALU.add
                                        ).then_inc(xs_ready, 1)

            def h_low(i, pair, u):
                pool.wait_ge(h_hi_ready, units(i, pair, u + 1))
                nc.gpsimd.tensor_tensor(h_lo[:, u, :], h[:, u % 2, :], h_hi[:, u, :].bitcast(F32),
                                        ALU.subtract).then_inc(h_lo_ready, 1)

            def run(i, k):
                ffn = k >= 2
                pair = k - 2 - k % 2
                inverse_std(i, k + 2, 0, ln1_step, ln1_ready)
                products(i, k + 1, 0)
                products(i, k + 1, 1)
                split_T(i, k + 1)
                add_skip(i, k + 1)
                if ffn:
                    h_low(i, pair, 0 if k % 2 == 0 else 4)
                skip_terms(i, k + 2)
                if ffn and k % 2 == 0:
                    for u in range(1, 4):
                        h_low(i, pair, u)
                inverse_std(i, k, 1, ln2_step, ln2_ready)

            run.engine = mybir.EngineType.Pool
            steps(run)

        @block.scalar
        def _(act):
            def times_bias(i, k):
                if not has(i, k):
                    return
                need(act, vbc_ready, count(i, k - 2, 1, 1))
                act.wait_ge(v_ready, count(i, k, 1, 1))
                nc.scalar.activation(vb[:, k % 2, :], v[:, k % 2, :], ACT.Copy, scale=bias(k)
                                     ).then_inc(vb_ready, 1)

            def copy_vT(i, k):
                if not has(i, k):
                    return
                act.wait_ge(vT_done, count(i, k, 1, 1))
                need(act, kv_ready, count(i, k - 2, MB, MB))
                nc.scalar.activation(vT[:, k % 2, :], turn_ps[:, 0:L], ACT.Copy).then_inc(vT_ready, 1)

            def kv_high(i, k, m):
                if not has(i, k):
                    return
                act.wait_ge(kv_ready, count(i, k, MB, m + 1))
                need(act, conv_done, count(i, k - 2, MB, MB))
                nc.scalar.activation(kv_hi[:, k % 2, m, :], kv[:, m, :], ACT.Copy).then_inc(kv_hi_ready, 1)

            def T_high(i, k):
                if not has(i, k):
                    return
                lap = 16 * (i + k // SLOTS + 1) if isinstance(i, int) else (i + (k // SLOTS + 1)) * 16
                act.wait_ge(in_loaded[k % SLOTS], lap)
                need(act, conv_done, count(i, k - 2, MB, MB))
                nc.scalar.activation(T_hi[:, k % 2, :], T(k), ACT.Copy).then_inc(T_hi_ready, 1)

            def xT_high(i, k):
                if not has(i, k):
                    return
                act.wait_ge(xT_done, count(i, k, 1, 1))
                nc.scalar.activation(xT_hi[:, :, (k % 2) * P:(k % 2 + 1) * P],
                                     turn_ps[:, 0:L].rearrange("p (c n) -> p c n", c=KC), ACT.Copy
                                     ).then_inc(xT_hi_ready, 1)

            def silu(i, pair, u):
                rows = REST if u == FULL else P
                lo = P - rows
                act.wait_ge(gate_done, units(i, pair, u + 1))
                need(act, h_ready, units(i, pair, u - 1 + PAD))
                nc.scalar.activation(gate[lo:P, u % 2, :], gate_ps[0:rows, 0:TOK], ACT.Silu,
                                     scale=scal[0:rows, GS + u:GS + u + 1]).then_inc(silu_ready, 1)

            def h_high(i, pair, u):
                lo = P - REST if u == FULL else 0
                act.wait_ge(h_ready, units(i, pair, u + 1 + PAD))
                nc.scalar.activation(h_hi[lo:P, u, :], h[lo:P, u % 2, :], ACT.Copy).then_inc(h_hi_ready, 1)

            def run(i, k):
                ffn = k >= 2
                pair = k - 2 - k % 2
                if k == -2:
                    act.wait_ge(scal_loaded, 16)
                    nc.scalar.activation(tanh_g[:, :], scal[:, GX:GF + 1], ACT.Tanh).then_inc(tanh_ready, 1)
                if k % 2 == 0:
                    xT_high(i, k - 1)
                T_high(i, k + 1)
                kv_high(i, k + 1, 0)
                times_bias(i, k + 2)
                if ffn and k % 2 == 0:
                    copy_vT(i, k + 2)
                    silu(i, pair, 0)
                    silu(i, pair, 1)
                    h_high(i, pair, 0)
                    kv_high(i, k + 1, 1)
                    silu(i, pair, 2)
                    h_high(i, pair, 1)
                    silu(i, pair, 3)
                    h_high(i, pair, 2)
                    h_high(i, pair, 3)
                elif ffn:
                    copy_vT(i, k + 2)
                    silu(i, pair, 4)
                    kv_high(i, k + 1, 1)
                    h_high(i, pair, 4)
                    silu(i, pair, 5)
                    xT_high(i, k - 1)
                    h_high(i, pair, 5)
                else:
                    copy_vT(i, k + 2)
                    kv_high(i, k + 1, 1)
                    if k % 2 == 1:
                        xT_high(i, k - 1)
                if k == 0:
                    act.wait_ge(wgu_loaded, 16)
                    nc.scalar.activation(wgu_hi[:, :, :], wgu[:, :, :], ACT.Copy).then_inc(wgu_hi_ready, 1)
                if k == 1:
                    act.wait_ge(wd_scaled, 1)
                    nc.scalar.activation(wd_hi[:, :, :], wd[:, :, :], ACT.Copy).then_inc(wd_hi_ready, 1)

            run.engine = mybir.EngineType.Activation
            steps(run)

        @block.vector
        def _(dve):
            nc.vector.memset(wd[:, FULL, :], 0.0).then_inc(zero_ready, 1)
            nc.vector.memset(h_hi[0:P - REST, FULL, :].bitcast(F32), 0.0).then_inc(h_ready, 1)
            for s in range(2):
                nc.vector.memset(res[:, s, :], 0.0).then_inc(res_free[s], 16)
            nc.vector.memset(h_lo[0:P - REST, FULL, :].bitcast(F32), 0.0).then_inc(h_ready, 1)

            def mean_var(i, k, which, step):
                nc.vector.bn_aggr(mv[:, which, :], stats[:, which, :]).then_inc(step, 1)
                dve.wait_ge(step, count(i, k, 3, 2))
                nc.vector.tensor_scalar(var_eps[:, which, :], mv[:, which, 1:2], EPS, None, ALU.add
                                        ).then_inc(step, 1)

            def normalize1(i, k):
                if not has(i, k):
                    return
                dve.wait_ge(ln1_ready, count(i, k, 1, 1))
                need(dve, vT_done, count(i, k - 2, 1, 1))
                need(dve, vb_ready, count(i, k - 2, 1, 1))
                nc.vector.tensor_scalar(v[:, k % 2, :], x_row(k), mv[:, 0, 0:1], rstd[:, 0, :], ALU.subtract,
                                        ALU.mult).then_inc(v_ready, 1)

            def normalize2(i, k):
                if not has(i, k):
                    return
                dve.wait_ge(ln2_ready, count(i, k, 1, 1))
                need(dve, xT_done, count(i, k - 2, 1, 1))
                nc.vector.tensor_scalar(xn[:, k % 2, :], x1[:, k % SLOTS, :], mv[:, 1, 0:1], rstd[:, 1, :],
                                        ALU.subtract, ALU.mult).then_inc(xn_ready, 1)

            def stats1(i, k):
                if not has(i, k):
                    return
                lap = 16 * (i + k // SLOTS + 1) if isinstance(i, int) else (i + (k // SLOTS + 1)) * 16
                dve.wait_ge(in_loaded[k % SLOTS], lap)
                nc.vector.bn_stats(stats[:, 0, :], x_row(k)).then_inc(ln1_step, 1)
                need(dve, v_ready, count(i, k - 1, 1, 1))
                dve.wait_ge(ln1_step, count(i, k, 3, 1))

            def mean_var1(i, k):
                if has(i, k):
                    mean_var(i, k, 0, ln1_step)

            def kv_low(i, k, m):
                if not has(i, k):
                    return
                dve.wait_ge(kv_hi_ready, count(i, k, MB, m + 1))
                nc.vector.tensor_tensor(kv_lo[:, k % 2, m, :], kv[:, m, :], kv_hi[:, k % 2, m, :].bitcast(F32),
                                        ALU.subtract).then_inc(kv_lo_ready, 1)

            def times_c(i, k, m):
                if not has(i, k):
                    return
                dve.wait_ge(conv_done, count(i, k, MB, m + 1))
                need(dve, mix_done, count(i, k - 1, 1, 1))
                nc.vector.tensor_tensor(by_ibj(z[:, m, :]), by_ibj(conv[:, m, :]), over_j(c_T(k, m)),
                                        ALU.mult).then_inc(z_ready, 1)

            def skip_product(i, k):
                if not has(i, k):
                    return
                dve.wait_ge(skip_done, count(i, k, 1, 1))
                need(dve, xs_ready, count(i, k - 2, 1, 1))
                if isinstance(i, int) and k == 0:
                    dve.wait_ge(tanh_ready, 1)
                nc.vector.scalar_tensor_tensor(out=skip[:, k % 2, :], in0=turn_ps[:, 0:L], scalar=tanh_g[:, 0:1],
                                               in1=c_row(k), op0=ALU.mult, op1=ALU.mult).then_inc(skip_ready, 1)

            def residual1(i, k):
                if not has(i, k):
                    return
                dve.wait_ge(mix_done, count(i, k, 1, 1))
                dve.wait_ge(xs_ready, count(i, k, 1, 1))
                nc.vector.scalar_tensor_tensor(out=x1[:, k % SLOTS, :], in0=out_ps[:, 0:L], scalar=tanh_g[:, 0:1],
                                               in1=xs[:, k % SLOTS, :], op0=ALU.mult, op1=ALU.add
                                               ).then_inc(x1_ready, 1)

            def stats2(i, k):
                if not has(i, k):
                    return
                dve.wait_ge(x1_ready, count(i, k, 1, 1))
                need(dve, xn_ready, count(i, k - 1, 1, 1))
                nc.vector.bn_stats(stats[:, 1, :], x1[:, k % SLOTS, :]).then_inc(ln2_step, 1)
                dve.wait_ge(ln2_step, count(i, k, 3, 1))

            def mean_var2(i, k):
                if has(i, k):
                    mean_var(i, k, 1, ln2_step)

            def xT_low(i, k):
                if not has(i, k):
                    return
                dve.wait_ge(xT_hi_ready, count(i, k, 1, 1))
                sl = slice((k % 2) * P, (k % 2 + 1) * P)
                nc.vector.tensor_tensor(xT_lo[:, :, sl], turn_ps[:, 0:L].rearrange("p (c n) -> p c n", c=KC),
                                        xT_hi[:, :, sl].bitcast(F32), ALU.subtract).then_inc(xT_lo_ready, 1)

            def times_up(i, pair, u):
                lo = P - REST if u == FULL else 0
                ps = gate_ps if u == FULL else up_ps
                if u < FULL:
                    dve.wait_ge(up_done, i * (2 * FULL) + (pair // 2 * FULL + u + 1))
                dve.wait_ge(silu_ready, units(i, pair, u + 1))
                if u >= 2 or isinstance(i, int):
                    need(dve, h_lo_ready, i * (2 * FULL) + (pair // 2 * FULL + max(u - 1, 0)))
                nc.vector.scalar_tensor_tensor(out=h[lo:P, u % 2, :], in0=ps[lo:P, 0:TOK],
                                               scalar=scal[lo:P, US + u:US + u + 1], in1=gate[lo:P, u % 2, :],
                                               op0=ALU.mult, op1=ALU.mult).then_inc(h_ready, 1)

            def h_low_rest(i, pair):
                dve.wait_ge(h_hi_ready, units(i, pair, NU))
                nc.vector.tensor_tensor(h_lo[P - REST:P, FULL, :], h[P - REST:P, FULL % 2, :],
                                        h_hi[P - REST:P, FULL, :].bitcast(F32), ALU.subtract
                                        ).then_inc(h_rest_ready, 1)

            def residual2(i, pair, s):
                tile = pair + s
                dve.wait_ge(down_done, count(i, tile, 1, 1))
                dve.wait_ge(res_free[s], (i * 2 + (pair // 2 + 1)) * 16)
                ps = out_ps if s == 0 else up_ps
                nc.vector.tensor_tensor(res[:, s, :], ps[:, 0:L], x1[:, tile % SLOTS, :], ALU.add
                                        ).then_inc(res_ready, 1)

            def run(i, k):
                ffn = k >= 2
                pair = k - 2 - k % 2
                if k == 1:
                    dve.wait_ge(wd_loaded, 3 * 16)
                    dve.wait_ge(tanh_ready, 1)
                    nc.vector.tensor_scalar(wd_s[:, :], wd_s[:, :], tanh_g[:, 1:2], None, ALU.mult
                                            ).then_inc(wd_s_ready, 1)
                    dve.wait_ge(wd_s_ready, 1)
                    nc.vector.tensor_tensor(wd[:, :, :], wd[:, :, :], wd_s[:, :].unsqueeze(1)
                                            .broadcast_to([P, NU, L]), ALU.mult).then_inc(wd_scaled, 1)
                stats1(i, k + 2)
                times_c(i, k, 0)
                mean_var1(i, k + 2)
                if k % 2 == 0:
                    xT_low(i, k - 1)
                normalize1(i, k + 2)
                kv_low(i, k + 1, 0)
                times_c(i, k, 1)
                if ffn and k % 2 == 0:
                    times_up(i, pair, 0)
                    times_up(i, pair, 1)
                    kv_low(i, k + 1, 1)
                    residual1(i, k)
                    stats2(i, k)
                    times_up(i, pair, 2)
                    mean_var2(i, k)
                    times_up(i, pair, 3)
                    normalize2(i, k)
                    skip_product(i, k + 2)
                elif ffn:
                    times_up(i, pair, 4)
                    kv_low(i, k + 1, 1)
                    times_up(i, pair, 5)
                    xT_low(i, k - 1)
                    residual1(i, k)
                    stats2(i, k)
                    skip_product(i, k + 2)
                    mean_var2(i, k)
                    h_low_rest(i, pair)
                    residual2(i, pair, 0)
                    residual2(i, pair, 1)
                    normalize2(i, k)
                else:
                    kv_low(i, k + 1, 1)
                    if k % 2 == 1:
                        xT_low(i, k - 1)
                    residual1(i, k)
                    stats2(i, k)
                    skip_product(i, k + 2)
                    mean_var2(i, k)
                    normalize2(i, k)
                if k == 0:
                    dve.wait_ge(wgu_hi_ready, 1)
                    nc.vector.tensor_tensor(wgu_lo[:, :, :], wgu[:, :, :], wgu_hi[:, :, :].bitcast(F32),
                                            ALU.subtract).then_inc(wgu_lo_ready, 1)
                if k == 1:
                    dve.wait_ge(wd_hi_ready, 1)
                    nc.vector.tensor_tensor(wd_lo[:, :, :], wd[:, :, :], wd_hi[:, :, :].bitcast(F32),
                                            ALU.subtract).then_inc(wd_lo_ready, 1)

            run.engine = mybir.EngineType.DVE
            steps(run)

        @block.tensor
        def _(pe):
            def split_product(dest, w_hi, w_lo, a_hi, a_lo, first, last):
                nc.tensor.matmul(dest, w_hi, a_hi, start=first, stop=False)
                nc.tensor.matmul(dest, w_hi, a_lo, start=False, stop=False)
                return nc.tensor.matmul(dest, w_lo, a_hi, start=False, stop=last)

            def convolve(i, k, lb):
                if not has(i, k):
                    return
                if lb == 0:
                    pe.wait_ge(T_lo_ready, count(i, k, 1, 1))
                    pe.wait_ge(T_hi_ready, count(i, k, 1, 1))
                pe.wait_ge(kv_hi_ready, count(i, k, MB, lb + 1))
                pe.wait_ge(kv_lo_ready, count(i, k, MB, lb + 1))
                need(pe, z_ready, count(i, k - 1, MB, lb + 1))
                for half in range(PAIRS // BANK):
                    sl = slice(half * BANK, (half + 1) * BANK)
                    for m in range(lb + 1):
                        cols = slice((lb - m) * P, (lb - m + 1) * P)
                        last = split_product(conv[:, lb, sl], T_hi[:, k % 2, cols], T_lo[:, k % 2, cols],
                                             kv_hi[:, k % 2, m, sl], kv_lo[:, k % 2, m, sl], m == 0, m == lb)
                last.then_inc(conv_done, 1)

            def sum_heads(i, k, lb):
                if not has(i, k):
                    return
                pe.wait_ge(z_ready, count(i, k, MB, lb + 1))
                if lb == 0:
                    need(pe, x1_ready, count(i, k - 1, 1, 1))
                for n in range(NH):
                    last = nc.tensor.matmul(out_ps[:, lb * P:(lb + 1) * P], z[:, lb, n * P:(n + 1) * P],
                                            ident[:, :], start=(n == 0), stop=(n == NH - 1), is_transpose=True)
                if lb == MB - 1:
                    last.then_inc(mix_done, 1)

            def turn_v(i, k):
                if not has(i, k):
                    return
                pe.wait_ge(v_ready, count(i, k, 1, 1))
                if isinstance(i, int) and k == 0:
                    pe.wait_ge(ident_ready, 1)
                need(pe, skip_ready, count(i, k - 1, 1, 1))
                if k % 2 == 0:
                    need(pe, xT_lo_ready, count(i, k - 3, 1, 1))
                for m in range(MB):
                    last = nc.tensor.transpose(turn_ps[:, m * P:(m + 1) * P], v[:, k % 2, m * P:(m + 1) * P],
                                               ident[:, :])
                last.then_inc(vT_done, 1)

            def turn_x(i, k):
                if not has(i, k):
                    return
                pe.wait_ge(xn_ready, count(i, k, 1, 1))
                if k % 2 == 1:
                    need(pe, skip_ready, min(count(i, k + 2, 1, 1), H) if isinstance(i, int)
                         else count(i, k + 2, 1, 1))
                else:
                    need(pe, vT_ready, min(count(i, k + 3, 1, 1), H) if isinstance(i, int)
                         else count(i, k + 3, 1, 1))
                for m in range(KC):
                    last = nc.tensor.transpose(turn_ps[:, m * P:(m + 1) * P], xn[:, k % 2, m * P:(m + 1) * P],
                                               ident[:, :])
                last.then_inc(xT_done, 1)

            def sum_skip(i, k):
                if not has(i, k):
                    return
                pe.wait_ge(vbc_ready, count(i, k, 1, 1))
                if isinstance(i, int) and k == 0:
                    pe.wait_ge(same_b_ready, 1)
                pe.wait_ge(vT_ready, count(i, k, 1, 1))
                if k % 2 == 1:
                    need(pe, xT_lo_ready, count(i, k - 3, 1, 1))
                nc.tensor.matmul(turn_ps[:, 0:L], same_b[:, :], vbc[:, k % 2, :], start=True, stop=True
                                 ).then_inc(skip_done, 1)

            def gate_up_chunk(dest, at, w):
                for c in range(KC):
                    last = split_product(dest, wgu_hi[:, c, at:at + w], wgu_lo[:, c, at:at + w],
                                         xT_hi[:, c, :], xT_lo[:, c, :], c == 0, c == KC - 1)
                return last

            def unit(i, pair, u):
                if u == 0:
                    pe.wait_ge(xT_hi_ready, count(i, pair + 1, 1, 1))
                    pe.wait_ge(xT_lo_ready, count(i, pair + 1, 1, 1))
                if u == 0:
                    need(pe, h_ready, units(i, pair, PAD))
                else:
                    pe.wait_ge(silu_ready, units(i, pair, u))
                gate_up_chunk(gate_ps[:, 0:TOK], 2 * u * P, P).then_inc(gate_done, 1)
                if u < FULL:
                    need(pe, h_ready, units(i, pair, u + PAD))
                    gate_up_chunk(up_ps[:, 0:TOK], (2 * u + 1) * P, P).then_inc(up_done, 1)

            def down(i, pair, s):
                have = units(i, pair, NU)
                if s == 0:
                    pe.wait_ge(h_hi_ready, have)
                    pe.wait_ge(h_lo_ready, i * (2 * FULL) + (pair // 2 * FULL + FULL))
                    pe.wait_ge(h_rest_ready, i * 2 + (pair // 2 + 1))
                    if has(i, pair + 3):
                        pe.wait_ge(x1_ready, count(i, pair + 3, 1, 1))
                    else:
                        pe.wait_ge(x1_ready, H)
                dest = (out_ps if s == 0 else up_ps)[:, 0:L]
                sl = slice(s * P, (s + 1) * P)
                for u in range(NU):
                    nc.tensor.matmul(dest, h_hi[:, u, sl], wd_hi[:, u, :], start=(u == 0), stop=False)
                    nc.tensor.matmul(dest, h_hi[:, u, sl], wd_lo[:, u, :], start=False, stop=False)
                    last = nc.tensor.matmul(dest, h_lo[:, u, sl], wd_hi[:, u, :], start=False, stop=(u == NU - 1))
                last.then_inc(down_done, 1)

            def run(i, k):
                ffn = k >= 2
                pair = k - 2 - k % 2
                convolve(i, k, 0)
                if k % 2 == 0:
                    turn_x(i, k - 1)
                convolve(i, k, 1)
                turn_v(i, k + 2)
                if k % 2 == 0:
                    if ffn:
                        unit(i, pair, 0)
                    sum_heads(i, k, 0)
                    if ffn:
                        unit(i, pair, 1)
                    sum_heads(i, k, 1)
                    if ffn:
                        unit(i, pair, 2)
                    sum_skip(i, k + 2)
                    if ffn:
                        unit(i, pair, 3)
                else:
                    if ffn:
                        unit(i, pair, 4)
                    sum_heads(i, k, 0)
                    if ffn:
                        unit(i, pair, 5)
                    turn_x(i, k - 1)
                    sum_heads(i, k, 1)
                    sum_skip(i, k + 2)
                    if ffn:
                        down(i, pair, 0)
                        down(i, pair, 1)
                if k == 1:
                    pe.wait_ge(wgu_hi_ready, 1)
                    pe.wait_ge(wgu_lo_ready, 1)
                    pe.wait_ge(wd_hi_ready, 1)
                    pe.wait_ge(wd_lo_ready, 1)

            run.engine = mybir.EngineType.PE
            steps(run)


def kernel(**inputs):
    import numpy as np
    import concourse.bacc as bacc
    from concourse.bass_utils import run_bass_kernel_spmd

    def tiles(a):
        return a.reshape(B, H, NH, L).transpose(1, 0, 2, 3).reshape(H, P, L)

    x, c = tiles(np.asarray(inputs["x"])), tiles(np.asarray(inputs["ctx_2048"]))
    cT = c.reshape(H, P, MB, P).transpose(0, 3, 2, 1).reshape(H, P, L)
    bias = np.broadcast_to(np.asarray(inputs["fside_S2_0"]).reshape(H, 1, NH), (H, B, NH)).reshape(H, P, 1)
    k_padded = np.concatenate([np.zeros((H, P - 1), np.float32), np.asarray(inputs["L0_xattn_k"])], axis=1)
    toeplitz = np.stack([k_padded[:, P - 1 - m:P - 1 - m + L] for m in range(P)], axis=1)
    packed = np.concatenate([x, c, cT, toeplitz, bias, np.zeros((H, P, PACK - BIAS - 1), np.float32)], axis=2).reshape(H * P, PACK)

    def columns(s, low):
        a = np.zeros((P, NU), np.float32)
        a[:, :FULL] = s[:FULL * P].reshape(FULL, P).T
        a[low:low + REST, FULL] = s[FULL * P:]
        return a

    gates = np.concatenate([np.asarray(inputs["g_xattn"]), np.asarray(inputs["g_ffn"])])
    scalars = np.concatenate([np.broadcast_to(gates, (P, 2)),
                              columns(np.asarray(inputs["L0_ffn_gate_s"]), 0),
                              columns(np.asarray(inputs["L0_ffn_up_s"]), P - REST)], axis=1)
    gw, uw = np.asarray(inputs["L0_ffn_gate_w"]), np.asarray(inputs["L0_ffn_up_w"])
    rows = []
    for u in range(NU):
        rows += [gw[u * P:(u + 1) * P], uw[u * P:(u + 1) * P]]
    gate_up = np.concatenate(rows).T.reshape(KC, P, GU).transpose(1, 0, 2)
    down = np.asarray(inputs["L0_ffn_down_w"]).T
    down_s = np.broadcast_to(np.asarray(inputs["L0_ffn_down_s"]), (P, L))

    arrays, args = {}, []
    nc = bacc.Bacc("TRN2", target_bir_lowering=False, num_devices=1)
    for name, a in (("packed", packed), ("scalars", scalars),
                    ("gate_up", gate_up), ("down", down), ("down_s", down_s)):
        arrays[name] = np.ascontiguousarray(a)
        args.append(nc.dram_tensor(name, arrays[name].shape, F32, kind="ExternalInput").ap())
    args.append(nc.dram_tensor("out", (H * P, L), F32, kind="ExternalOutput").ap())
    flamingo(nc, *args)
    r = run_bass_kernel_spmd(nc, [arrays], core_ids=[0])
    y = r.results[0]["out"]
    return y.reshape(H, B, NH, L).transpose(1, 0, 2, 3).reshape(B, D, L)
```

```python
from contextlib import ExitStack

import concourse.bass as bass
from concourse import mybir

B, D, L = 16, 128, 256
NH = 8
H = D // NH
INTER = 704
P = 128
MB = L // P
EPS = 1e-5

PAIRS = NH * B * NH
BANK = 512
KC = L // P
FULL = INTER // P
REST = INTER - FULL * P
NU = FULL + 1
GU = 2 * INTER
TOK = 2 * P
SLOTS = 4
PACK = 4 * L + 4
BIAS = 4 * L

WARM = 5
PAD = 2

GX, GF, GS, US = 0, 1, 2, 2 + NU
SCAL = 2 + 2 * NU

F32 = mybir.dt.float32
F32R = mybir.dt.float32r
ALU = mybir.AluOpType
ACT = mybir.ActivationFunctionType


def count(i, k, per=1, done=0):
    return i * (SLOTS * per) + (k * per + done)


def units(i, pair, done):
    return i * (2 * NU) + (pair // 2 * NU + done)


def has(i, k):
    return not isinstance(i, int) or 0 <= SLOTS * i + k < H


def need(eng, sem, value):
    if not isinstance(value, int) or value > 0:
        eng.wait_ge(sem, value)


def flamingo(nc, packed, scalars, gate_up_w, down_w, down_s, out):
    with ExitStack() as ctx:
        def sb(name, shape, dt=F32):
            return ctx.enter_context(nc.sbuf_tensor(name, shape, dt))

        def sem(name):
            return ctx.enter_context(nc.semaphore(name))

        ins = sb("ins", [P, SLOTS, PACK])
        xs = sb("xs", [P, SLOTS, L])
        x1 = sb("x1", [P, SLOTS, L])
        stats = sb("stats", [P, 2, 6])
        mv = sb("mv", [P, 2, 2])
        var_eps = sb("var_eps", [P, 2, 1])
        rstd = sb("rstd", [P, 2, 1])
        carrier = sb("carrier", [P, 2])
        minus_half = sb("minus_half", [P, 1])
        v = sb("v", [P, 2, L])
        vb = sb("vb", [P, 2, L])
        vbc = sb("vbc", [P, 2, L])
        skip = sb("skip", [P, 2, L])
        vT = sb("vT", [P, 2, MB * P])
        kv = sb("kv", [P, MB, PAIRS])
        kv_hi = sb("kv_hi", [P, 2, MB, PAIRS], F32R)
        kv_lo = sb("kv_lo", [P, 2, MB, PAIRS], F32R)
        T_hi = sb("T_hi", [P, 2, L], F32R)
        T_lo = sb("T_lo", [P, 2, L], F32R)
        z = sb("z", [P, MB, PAIRS])
        xn = sb("xn", [P, 2, L])
        xT_hi = sb("xT_hi", [P, KC, TOK], F32R)
        xT_lo = sb("xT_lo", [P, KC, TOK], F32R)
        gate = sb("gate", [P, 2, TOK])
        h = sb("h", [P, 2, TOK])
        h_hi = sb("h_hi", [P, NU, TOK], F32R)
        h_lo = sb("h_lo", [P, NU, TOK], F32R)
        res = sb("res", [P, 2, L])
        scal = sb("scal", [P, SCAL])
        tanh_g = sb("tanh_g", [P, 2])
        wgu = sb("wgu", [P, KC, GU])
        wgu_hi = sb("wgu_hi", [P, KC, GU], F32R)
        wgu_lo = sb("wgu_lo", [P, KC, GU], F32R)
        wd = sb("wd", [P, NU, L])
        wd_s = sb("wd_s", [P, L])
        wd_hi = sb("wd_hi", [P, NU, L], F32R)
        wd_lo = sb("wd_lo", [P, NU, L], F32R)
        ident = sb("ident", [P, P])
        same_b = sb("same_b", [P, P])

        conv = ctx.enter_context(nc.psum_tensor("conv", [P, MB, PAIRS], F32))
        unit_ps = ctx.enter_context(nc.psum_tensor("unit_ps", [P, 2, BANK], F32))
        turn_ps = ctx.enter_context(nc.psum_tensor("turn_ps", [P, BANK], F32))
        out_ps = ctx.enter_context(nc.psum_tensor("out_ps", [P, BANK], F32))

        in_loaded = [sem(f"in_loaded{s}") for s in range(SLOTS)]
        scal_loaded, wgu_loaded, wd_loaded = sem("scal_loaded"), sem("wgu_loaded"), sem("wd_loaded")
        first_x_loaded = sem("first_x_loaded")
        ident_ready, same_b_ready, const_step = sem("ident_ready"), sem("same_b_ready"), sem("const_step")
        tanh_ready, zero_ready = sem("tanh_ready"), sem("zero_ready")
        wgu_hi_ready, wgu_lo_ready = sem("wgu_hi_ready"), sem("wgu_lo_ready")
        wd_s_ready, wd_scaled, wd_hi_ready, wd_lo_ready = (
            sem("wd_s_ready"), sem("wd_scaled"), sem("wd_hi_ready"), sem("wd_lo_ready"))
        ln1_step, ln1_ready, half_ready = sem("ln1_step"), sem("ln1_ready"), sem("half_ready")
        v_ready, vb_ready, vbc_ready = sem("v_ready"), sem("vb_ready"), sem("vbc_ready")
        vT_done, vT_ready = sem("vT_done"), sem("vT_ready")
        skip_done, skip_ready, xs_ready = sem("skip_done"), sem("skip_ready"), sem("xs_ready")
        kv_ready, kv_hi_ready, kv_lo_ready = sem("kv_ready"), sem("kv_hi_ready"), sem("kv_lo_ready")
        T_hi_ready, T_lo_ready = sem("T_hi_ready"), sem("T_lo_ready")
        conv_done, z_ready, mix_done, x1_ready = (
            sem("conv_done"), sem("z_ready"), sem("mix_done"), sem("x1_ready"))
        ln2_step, ln2_ready = sem("ln2_step"), sem("ln2_ready")
        xn_ready, xT_done, xT_hi_ready, xT_lo_ready = (
            sem("xn_ready"), sem("xT_done"), sem("xT_hi_ready"), sem("xT_lo_ready"))
        unit_done, silu_ready = sem("unit_done"), sem("silu_ready")
        h_ready, h_hi_ready, h_lo_ready, h_rest_ready = (
            sem("h_ready"), sem("h_hi_ready"), sem("h_lo_ready"), sem("h_rest_ready"))
        down_done, res_ready = sem("down_done"), sem("res_ready")
        res_free = [sem(f"res_free{s}") for s in range(2)]

        def x_row(k):
            return ins[:, k % SLOTS, 0:L]

        def c_row(k):
            return ins[:, k % SLOTS, L:2 * L]

        def c_T(k, m):
            return ins[:, k % SLOTS, 2 * L + m * P:2 * L + (m + 1) * P]

        def T(k):
            return ins[:, k % SLOTS, 3 * L:4 * L]

        def bias(k):
            return ins[:, k % SLOTS, BIAS:BIAS + 1]

        def over_j(a):
            return a.rearrange("p (b i) -> p i b", i=NH).unsqueeze(3).broadcast_to([P, NH, B, NH])

        def over_i(a):
            return a.unsqueeze(1).broadcast_to([P, NH, P])

        def by_i(a):
            return a.rearrange("p (i n) -> p i n", i=NH)

        def by_ibj(a):
            return a.rearrange("p (i b j) -> p i b j", i=NH, b=B)

        def steps(run):
            for k in range(-2, 2 + SLOTS):
                run(0, k)
            with nc.Fori(1, (H - 4) // SLOTS, engines=[run.engine]) as i:
                for k in range(2, 2 + SLOTS):
                    run(i, k)
            for k in range(H - 2, H + 2):
                run(0, k)

        block = ctx.enter_context(nc.Block())

        @block.sync
        def _(sp):
            def load(i, k):
                if not has(i, k):
                    return
                row = (i * SLOTS + k) * P
                need(sp, x1_ready, count(i, k - SLOTS, 1, 1))
                sp.dma_start(ins[:, k % SLOTS, :], packed[bass.ds(row, P), :]
                             ).then_inc(in_loaded[k % SLOTS], 16)

            def store(i, k):
                for s in range(2):
                    row = (i * SLOTS + k + s) * P
                    sp.wait_ge(res_ready, count(i, k + s, 1, 1))
                    sp.dma_start(out[bass.ds(row, P), :], res[:, s, :]).then_inc(res_free[s], 16)

            sp.dma_start(ins[:, 0, 0:L], packed[0:P, 0:L]).then_inc(first_x_loaded, 16)
            sp.dma_start(ins[:, 0, L:PACK], packed[0:P, L:PACK]).then_inc(in_loaded[0], 16)
            sp.dma_start(scal[:, :], scalars).then_inc(scal_loaded, 16)
            load(0, 1)
            load(0, 2)
            sp.dma_start(wgu[:, :, :], gate_up_w).then_inc(wgu_loaded, 16)
            load(0, 3)
            sp.wait_ge(zero_ready, 1)
            sp.dma_start(wd[:, 0:FULL, :], down_w[0:FULL * P, :].rearrange("(c p) n -> p c n", p=P)
                         ).then_inc(wd_loaded, 16)
            sp.dma_start(wd[P - REST:P, FULL, :], down_w[FULL * P:INTER, :]).then_inc(wd_loaded, 16)
            sp.dma_start(wd_s[:, :], down_s).then_inc(wd_loaded, 16)
            load(0, 4)
            load(0, 5)

            def turn(i, pair):
                load(i, pair + 6)
                load(i, pair + 7)
                store(i, pair)

            with nc.Fori(0, H // SLOTS - 2, engines=[mybir.EngineType.SP]) as i:
                turn(i, 0)
                turn(i, 2)
            for pair in range(H - 2 * SLOTS, H, 2):
                turn(0, pair)
            for s in range(2):
                sp.wait_ge(res_free[s], 16 * (H // 2 + 1))

        @block.gpsimd
        def _(pool):
            nc.gpsimd.memset(minus_half[:, :], -0.5).then_inc(half_ready, 1)
            nc.gpsimd.memset(ident[:, :], 0.0).then_inc(const_step, 1)
            nc.gpsimd.memset(same_b[:, :], 1.0).then_inc(const_step, 1)
            pool.wait_ge(const_step, 2)
            nc.gpsimd.affine_select(out=ident[:, :], in_=ident[:, :], compare_op=ALU.not_equal, fill=1.0, base=0,
                                    pattern=[[-1, P]], channel_multiplier=1).then_inc(ident_ready, 1)
            sb3 = same_b[:, :].rearrange("p (b j) -> p b j", j=NH)
            nc.gpsimd.affine_select(out=sb3, in_=sb3, compare_op=ALU.is_ge, fill=0.0, base=0,
                                    pattern=[[-NH, B], [0, NH]], channel_multiplier=1).then_inc(const_step, 1)
            pool.wait_ge(const_step, 3)
            nc.gpsimd.affine_select(out=sb3, in_=sb3, compare_op=ALU.is_ge, fill=0.0, base=NH - 1,
                                    pattern=[[NH, B], [0, NH]], channel_multiplier=-1).then_inc(same_b_ready, 1)

            def inverse_std(i, k, which, step, ready):
                if not has(i, k):
                    return
                if isinstance(i, int) and k == 0:
                    pool.wait_ge(half_ready, 1)
                pool.wait_ge(step, count(i, k, 4, 4))
                nc.gpsimd.tensor_tensor(rstd[:, which, :], var_eps[:, which, :], minus_half[:, :], ALU.pow
                                        ).then_inc(ready, 1)

            def products(i, k, m):
                if not has(i, k):
                    return
                if m == 0:
                    pool.wait_ge(vT_ready, count(i, k, 1, 1))
                need(pool, kv_lo_ready, count(i, k - 1, MB, m + 1))
                nc.gpsimd.tensor_tensor(by_ibj(kv[:, m, :]), over_j(vT[:, k % 2, m * P:(m + 1) * P]),
                                        c_T(k, m).rearrange("p (b j) -> p b j", j=NH).unsqueeze(1)
                                        .broadcast_to([P, NH, B, NH]), ALU.mult).then_inc(kv_ready, 1)

            def split_T(i, k):
                if not has(i, k):
                    return
                pool.wait_ge(T_hi_ready, count(i, k, 1, 1))
                nc.gpsimd.tensor_tensor(T_lo[:, k % 2, :], T(k), T_hi[:, k % 2, :].bitcast(F32),
                                        ALU.subtract).then_inc(T_lo_ready, 1)

            def skip_terms(i, k):
                if not has(i, k):
                    return
                pool.wait_ge(vb_ready, count(i, k, 1, 1))
                need(pool, skip_done, count(i, k - 2, 1, 1))
                nc.gpsimd.tensor_tensor(vbc[:, k % 2, :], vb[:, k % 2, :], c_row(k), ALU.mult
                                        ).then_inc(vbc_ready, 1)

            def add_skip(i, k):
                if not has(i, k):
                    return
                pool.wait_ge(skip_ready, count(i, k, 1, 1))
                need(pool, x1_ready, count(i, k - SLOTS, 1, 1))
                nc.gpsimd.tensor_tensor(xs[:, k % SLOTS, :], x_row(k), skip[:, k % 2, :], ALU.add
                                        ).then_inc(xs_ready, 1)

            def h_low(i, pair, u):
                pool.wait_ge(h_hi_ready, units(i, pair, u + 1))
                nc.gpsimd.tensor_tensor(h_lo[:, u, :], h[:, u % 2, :], h_hi[:, u, :].bitcast(F32),
                                        ALU.subtract).then_inc(h_lo_ready, 1)

            def run(i, k):
                ffn = k >= 2
                pair = k - 2 - k % 2
                once = isinstance(i, int) and k < SLOTS
                if k != 1:
                    products(i, k + 1, 0)
                inverse_std(i, k + 2, 0, ln1_step, ln1_ready)
                if ffn and k % 2 == 1:
                    h_low(i, pair, 3)
                if k == -1:
                    split_T(0, 0)
                    products(0, 0, 1)
                    skip_terms(0, 0)
                    skip_terms(0, 1)
                elif k >= 0:
                    products(i, k + 1, 1)
                    if ffn and k % 2 == 1:
                        h_low(i, pair, 4)
                    split_T(i, k + 1)
                    if k == 0:
                        add_skip(0, 0)
                    add_skip(i, k + 1)
                    skip_terms(i, k + 2)
                if k == 0:
                    products(0, 2, 0)
                if ffn and k % 2 == 0:
                    h_low(i, pair, 0)
                    h_low(i, pair, 1)
                    h_low(i, pair, 2)
                inverse_std(i, k, 1, ln2_step, ln2_ready)

            run.engine = mybir.EngineType.Pool
            steps(run)

        @block.scalar
        def _(act):
            def times_bias(i, k):
                if not has(i, k):
                    return
                need(act, vbc_ready, count(i, k - 2, 1, 1))
                act.wait_ge(v_ready, count(i, k, 1, 1))
                nc.scalar.activation(vb[:, k % 2, :], v[:, k % 2, :], ACT.Copy, scale=bias(k)
                                     ).then_inc(vb_ready, 1)

            def copy_vT(i, k):
                if not has(i, k):
                    return
                act.wait_ge(vT_done, count(i, k, 1, 1))
                need(act, kv_ready, count(i, k - 2, MB, MB))
                nc.scalar.activation(vT[:, k % 2, :], turn_ps[:, 0:L], ACT.Copy).then_inc(vT_ready, 1)

            def kv_high(i, k, m):
                if not has(i, k):
                    return
                act.wait_ge(kv_ready, count(i, k, MB, m + 1))
                need(act, conv_done, count(i, k - 2, MB, MB))
                nc.scalar.activation(kv_hi[:, k % 2, m, :], kv[:, m, :], ACT.Copy).then_inc(kv_hi_ready, 1)

            def T_high(i, k):
                if not has(i, k):
                    return
                lap = 16 * (i + k // SLOTS + 1) if isinstance(i, int) else (i + (k // SLOTS + 1)) * 16
                act.wait_ge(in_loaded[k % SLOTS], lap)
                need(act, conv_done, count(i, k - 2, MB, MB))
                nc.scalar.activation(T_hi[:, k % 2, :], T(k), ACT.Copy).then_inc(T_hi_ready, 1)

            def xT_high(i, k):
                if not has(i, k):
                    return
                act.wait_ge(xT_done, count(i, k, 1, 1))
                nc.scalar.activation(xT_hi[:, :, (k % 2) * P:(k % 2 + 1) * P],
                                     turn_ps[:, 0:L].rearrange("p (c n) -> p c n", c=KC), ACT.Copy
                                     ).then_inc(xT_hi_ready, 1)

            def silu(i, pair, u):
                rows = REST if u == FULL else P
                lo = P - rows
                act.wait_ge(unit_done, units(i, pair, u + 1))
                need(act, h_ready, units(i, pair, u - 1 + PAD))
                nc.scalar.activation(gate[lo:P, u % 2, :], unit_ps[0:rows, u % 2, 0:TOK], ACT.Silu,
                                     scale=scal[0:rows, GS + u:GS + u + 1]).then_inc(silu_ready, 1)

            def h_high(i, pair, u):
                lo = P - REST if u == FULL else 0
                act.wait_ge(h_ready, units(i, pair, u + 1 + PAD))
                nc.scalar.activation(h_hi[lo:P, u, :], h[lo:P, u % 2, :], ACT.Copy).then_inc(h_hi_ready, 1)

            def gate_up_high(c):
                nc.scalar.activation(wgu_hi[:, c, :], wgu[:, c, :], ACT.Copy).then_inc(wgu_hi_ready, 1)

            def run(i, k):
                ffn = k >= 2
                pair = k - 2 - k % 2
                once = isinstance(i, int) and k < SLOTS
                if k == -2:
                    act.wait_ge(scal_loaded, 16)
                    nc.scalar.activation(tanh_g[:, :], scal[:, GX:GF + 1], ACT.Tanh).then_inc(tanh_ready, 1)
                if k % 2 == 0:
                    xT_high(i, k - 1)
                T_high(i, k + 1)
                if ffn and k % 2 == 1:
                    silu(i, pair, 4)
                kv_high(i, k + 1, 0)
                times_bias(i, k + 2)
                if ffn and k % 2 == 1:
                    h_high(i, pair, 4)
                    copy_vT(i, k + 2)
                    silu(i, pair, 5)
                    xT_high(i, k - 1)
                    h_high(i, pair, 5)
                kv_high(i, k + 1, 1)
                if ffn and k % 2 == 0:
                    silu(i, pair, 0)
                    copy_vT(i, k + 2)
                    h_high(i, pair, 0)
                    silu(i, pair, 1)
                    h_high(i, pair, 1)
                    silu(i, pair, 2)
                    h_high(i, pair, 2)
                    silu(i, pair, 3)
                    h_high(i, pair, 3)
                elif not ffn:
                    copy_vT(i, k + 2)
                    if k % 2 == 1:
                        xT_high(i, k - 1)
                if k == -1:
                    act.wait_ge(wgu_loaded, 16)
                    gate_up_high(0)
                if k == 0:
                    gate_up_high(1)
                if once and k == 2:
                    act.wait_ge(wd_scaled, 1)
                    nc.scalar.activation(wd_hi[:, :, :], wd[:, :, :], ACT.Copy).then_inc(wd_hi_ready, 1)

            run.engine = mybir.EngineType.Activation
            steps(run)

        @block.vector
        def _(dve):
            nc.vector.memset(wd[:, FULL, :], 0.0).then_inc(zero_ready, 1)
            nc.vector.memset(h_hi[0:P - REST, FULL, :].bitcast(F32), 0.0).then_inc(h_ready, 1)
            for s in range(2):
                nc.vector.memset(res[:, s, :], 0.0).then_inc(res_free[s], 16)
            nc.vector.memset(h_lo[0:P - REST, FULL, :].bitcast(F32), 0.0).then_inc(h_ready, 1)

            def statistics(i, k, which, src, step):
                nc.vector.bn_stats(stats[:, which, :], src).then_inc(step, 1)
                dve.wait_ge(step, count(i, k, 4, 1))
                nc.vector.tensor_copy(carrier[:, which:which + 1], stats[:, which, 0:1]).then_inc(step, 1)
                nc.vector.bn_aggr(mv[:, which, :], stats[:, which, :]).then_inc(step, 1)
                dve.wait_ge(step, count(i, k, 4, 3))
                nc.vector.tensor_scalar(var_eps[:, which, :], mv[:, which, 1:2], EPS, None, ALU.add
                                        ).then_inc(step, 1)

            def normalize1(i, k):
                if not has(i, k):
                    return
                dve.wait_ge(ln1_ready, count(i, k, 1, 1))
                need(dve, vT_done, count(i, k - 2, 1, 1))
                need(dve, vb_ready, count(i, k - 2, 1, 1))
                nc.vector.tensor_scalar(v[:, k % 2, :], x_row(k), mv[:, 0, 0:1], rstd[:, 0, :], ALU.subtract,
                                        ALU.mult).then_inc(v_ready, 1)

            def normalize2(i, k):
                if not has(i, k):
                    return
                dve.wait_ge(ln2_ready, count(i, k, 1, 1))
                need(dve, xT_done, count(i, k - 2, 1, 1))
                nc.vector.tensor_scalar(xn[:, k % 2, :], x1[:, k % SLOTS, :], mv[:, 1, 0:1], rstd[:, 1, :],
                                        ALU.subtract, ALU.mult).then_inc(xn_ready, 1)

            def stats1(i, k):
                if not has(i, k):
                    return
                lap = 16 * (i + k // SLOTS + 1) if isinstance(i, int) else (i + (k // SLOTS + 1)) * 16
                if isinstance(i, int) and k == 0:
                    dve.wait_ge(first_x_loaded, 16)
                else:
                    dve.wait_ge(in_loaded[k % SLOTS], lap)
                need(dve, v_ready, count(i, k - 1, 1, 1))
                statistics(i, k, 0, x_row(k), ln1_step)

            def kv_low(i, k, m):
                if not has(i, k):
                    return
                dve.wait_ge(kv_hi_ready, count(i, k, MB, m + 1))
                nc.vector.tensor_tensor(kv_lo[:, k % 2, m, :], kv[:, m, :], kv_hi[:, k % 2, m, :].bitcast(F32),
                                        ALU.subtract).then_inc(kv_lo_ready, 1)

            def times_c(i, k, m):
                if not has(i, k):
                    return
                dve.wait_ge(conv_done, count(i, k, MB, m + 1))
                need(dve, mix_done, count(i, k - 1, 1, 1))
                nc.vector.tensor_tensor(by_ibj(z[:, m, :]), by_ibj(conv[:, m, :]), over_j(c_T(k, m)),
                                        ALU.mult).then_inc(z_ready, 1)

            def skip_product(i, k):
                if not has(i, k):
                    return
                dve.wait_ge(skip_done, count(i, k, 1, 1))
                need(dve, xs_ready, count(i, k - 2, 1, 1))
                if isinstance(i, int) and k == 0:
                    dve.wait_ge(tanh_ready, 1)
                nc.vector.scalar_tensor_tensor(out=skip[:, k % 2, :], in0=turn_ps[:, 0:L], scalar=tanh_g[:, 0:1],
                                               in1=c_row(k), op0=ALU.mult, op1=ALU.mult).then_inc(skip_ready, 1)

            def residual1(i, k):
                if not has(i, k):
                    return
                dve.wait_ge(mix_done, count(i, k, 1, 1))
                dve.wait_ge(xs_ready, count(i, k, 1, 1))
                nc.vector.scalar_tensor_tensor(out=x1[:, k % SLOTS, :], in0=out_ps[:, 0:L], scalar=tanh_g[:, 0:1],
                                               in1=xs[:, k % SLOTS, :], op0=ALU.mult, op1=ALU.add
                                               ).then_inc(x1_ready, 1)

            def stats2(i, k):
                if not has(i, k):
                    return
                dve.wait_ge(x1_ready, count(i, k, 1, 1))
                need(dve, xn_ready, count(i, k - 1, 1, 1))
                statistics(i, k, 1, x1[:, k % SLOTS, :], ln2_step)

            def xT_low(i, k):
                if not has(i, k):
                    return
                dve.wait_ge(xT_hi_ready, count(i, k, 1, 1))
                sl = slice((k % 2) * P, (k % 2 + 1) * P)
                nc.vector.tensor_tensor(xT_lo[:, :, sl], turn_ps[:, 0:L].rearrange("p (c n) -> p c n", c=KC),
                                        xT_hi[:, :, sl].bitcast(F32), ALU.subtract).then_inc(xT_lo_ready, 1)

            def times_up(i, pair, u):
                lo = P - REST if u == FULL else 0
                at = 0 if u == FULL else TOK
                dve.wait_ge(silu_ready, units(i, pair, u + 1))
                if u >= 2 or isinstance(i, int):
                    need(dve, h_lo_ready, i * (2 * FULL) + (pair // 2 * FULL + max(u - 1, 0)))
                nc.vector.scalar_tensor_tensor(out=h[lo:P, u % 2, :], in0=unit_ps[lo:P, u % 2, at:at + TOK],
                                               scalar=scal[lo:P, US + u:US + u + 1], in1=gate[lo:P, u % 2, :],
                                               op0=ALU.mult, op1=ALU.mult).then_inc(h_ready, 1)

            def h_low_rest(i, pair):
                dve.wait_ge(h_hi_ready, units(i, pair, NU))
                nc.vector.tensor_tensor(h_lo[P - REST:P, FULL, :], h[P - REST:P, FULL % 2, :],
                                        h_hi[P - REST:P, FULL, :].bitcast(F32), ALU.subtract
                                        ).then_inc(h_rest_ready, 1)

            def residual2(i, pair, s):
                tile = pair + s
                dve.wait_ge(down_done, count(i, tile, 1, 1))
                dve.wait_ge(res_free[s], (i * 2 + (pair // 2 + 1)) * 16)
                nc.vector.tensor_tensor(res[:, s, :], unit_ps[:, s, 0:L], x1[:, tile % SLOTS, :], ALU.add
                                        ).then_inc(res_ready, 1)

            def gate_up_low(c):
                dve.wait_ge(wgu_hi_ready, c + 1)
                nc.vector.tensor_tensor(wgu_lo[:, c, :], wgu[:, c, :], wgu_hi[:, c, :].bitcast(F32),
                                        ALU.subtract).then_inc(wgu_lo_ready, 1)

            def scale_down():
                dve.wait_ge(wd_loaded, 3 * 16)
                dve.wait_ge(tanh_ready, 1)
                nc.vector.tensor_scalar(wd_s[:, :], wd_s[:, :], tanh_g[:, 1:2], None, ALU.mult
                                        ).then_inc(wd_s_ready, 1)
                dve.wait_ge(wd_s_ready, 1)
                nc.vector.tensor_tensor(wd[:, :, :], wd[:, :, :], wd_s[:, :].unsqueeze(1)
                                        .broadcast_to([P, NU, L]), ALU.mult).then_inc(wd_scaled, 1)

            def down_low():
                dve.wait_ge(wd_hi_ready, 1)
                nc.vector.tensor_tensor(wd_lo[:, :, :], wd[:, :, :], wd_hi[:, :, :].bitcast(F32),
                                        ALU.subtract).then_inc(wd_lo_ready, 1)

            def run(i, k):
                ffn = k >= 2
                pair = k - 2 - k % 2
                once = isinstance(i, int) and k < SLOTS
                stats1(i, k + 2)
                if k == 0:
                    skip_product(0, 0)
                times_c(i, k, 0)
                if k % 2 == 0:
                    xT_low(i, k - 1)
                if ffn and k % 2 == 1:
                    times_up(i, pair, 4)
                normalize1(i, k + 2)
                kv_low(i, k + 1, 0)
                if k == 0:
                    skip_product(0, 1)
                times_c(i, k, 1)
                if ffn and k % 2 == 0:
                    times_up(i, pair, 0)
                if not ffn or k % 2 == 0:
                    kv_low(i, k + 1, 1)
                if k % 2 == 0:
                    if ffn:
                        times_up(i, pair, 1)
                    residual1(i, k)
                    stats2(i, k)
                    if ffn:
                        times_up(i, pair, 2)
                    if k >= 0:
                        skip_product(i, k + 2)
                    if ffn:
                        times_up(i, pair, 3)
                    normalize2(i, k)
                else:
                    if ffn:
                        times_up(i, pair, 5)
                    xT_low(i, k - 1)
                    if once and k == 1:
                        gate_up_low(0)
                    if once and k == 3:
                        down_low()
                    if ffn:
                        h_low_rest(i, pair)
                    residual1(i, k)
                    stats2(i, k)
                    if ffn:
                        kv_low(i, k + 1, 1)
                        residual2(i, pair, 0)
                    if k >= 0:
                        skip_product(i, k + 2)
                    normalize2(i, k)
                    if ffn:
                        residual2(i, pair, 1)
                if once and k == 1:
                    gate_up_low(1)
                if once and k == 2:
                    scale_down()

            run.engine = mybir.EngineType.DVE
            steps(run)

        @block.tensor
        def _(pe):
            def split_product(dest, w_hi, w_lo, a_hi, a_lo, first, last):
                nc.tensor.matmul(dest, w_hi, a_hi, start=first, stop=False)
                nc.tensor.matmul(dest, w_hi, a_lo, start=False, stop=False)
                return nc.tensor.matmul(dest, w_lo, a_hi, start=False, stop=last)

            def convolve(i, k, lb):
                if not has(i, k):
                    return
                if lb == 0:
                    pe.wait_ge(T_lo_ready, count(i, k, 1, 1))
                    pe.wait_ge(T_hi_ready, count(i, k, 1, 1))
                pe.wait_ge(kv_hi_ready, count(i, k, MB, lb + 1))
                pe.wait_ge(kv_lo_ready, count(i, k, MB, lb + 1))
                need(pe, z_ready, count(i, k - 1, MB, lb + 1))
                for half in range(PAIRS // BANK):
                    sl = slice(half * BANK, (half + 1) * BANK)
                    for m in range(lb + 1):
                        cols = slice((lb - m) * P, (lb - m + 1) * P)
                        last = split_product(conv[:, lb, sl], T_hi[:, k % 2, cols], T_lo[:, k % 2, cols],
                                             kv_hi[:, k % 2, m, sl], kv_lo[:, k % 2, m, sl], m == 0, m == lb)
                last.then_inc(conv_done, 1)

            def sum_heads(i, k, lb):
                if not has(i, k):
                    return
                pe.wait_ge(z_ready, count(i, k, MB, lb + 1))
                if lb == 0:
                    need(pe, x1_ready, count(i, k - 1, 1, 1))
                for n in range(NH):
                    last = nc.tensor.matmul(out_ps[:, lb * P:(lb + 1) * P], z[:, lb, n * P:(n + 1) * P],
                                            ident[:, :], start=(n == 0), stop=(n == NH - 1), is_transpose=True)
                if lb == MB - 1:
                    last.then_inc(mix_done, 1)

            def turn_v(i, k):
                if not has(i, k):
                    return
                pe.wait_ge(v_ready, count(i, k, 1, 1))
                if isinstance(i, int) and k == 0:
                    pe.wait_ge(ident_ready, 1)
                if isinstance(i, int) and k == 1:
                    pe.wait_ge(vT_ready, 1)
                else:
                    need(pe, skip_ready, count(i, k - 1, 1, 1))
                if k % 2 == 0:
                    need(pe, xT_lo_ready, count(i, k - 3, 1, 1))
                for m in range(MB):
                    last = nc.tensor.transpose(turn_ps[:, m * P:(m + 1) * P], v[:, k % 2, m * P:(m + 1) * P],
                                               ident[:, :])
                last.then_inc(vT_done, 1)

            def turn_x(i, k):
                if not has(i, k):
                    return
                pe.wait_ge(xn_ready, count(i, k, 1, 1))
                if k % 2 == 1:
                    need(pe, skip_ready, min(count(i, k + 2, 1, 1), H) if isinstance(i, int)
                         else count(i, k + 2, 1, 1))
                else:
                    need(pe, vT_ready, min(count(i, k + 3, 1, 1), H) if isinstance(i, int)
                         else count(i, k + 3, 1, 1))
                for m in range(KC):
                    last = nc.tensor.transpose(turn_ps[:, m * P:(m + 1) * P], xn[:, k % 2, m * P:(m + 1) * P],
                                               ident[:, :])
                last.then_inc(xT_done, 1)

            def sum_skip(i, k):
                if not has(i, k):
                    return
                pe.wait_ge(vbc_ready, count(i, k, 1, 1))
                if isinstance(i, int) and k == 0:
                    pe.wait_ge(same_b_ready, 1)
                if isinstance(i, int) and k == 0:
                    pe.wait_ge(vT_ready, 2)
                elif isinstance(i, int) and k == 1:
                    pe.wait_ge(skip_ready, 1)
                else:
                    pe.wait_ge(vT_ready, count(i, k, 1, 1))
                if k % 2 == 1:
                    need(pe, xT_lo_ready, count(i, k - 3, 1, 1))
                nc.tensor.matmul(turn_ps[:, 0:L], same_b[:, :], vbc[:, k % 2, :], start=True, stop=True
                                 ).then_inc(skip_done, 1)

            def gate_up_chunk(dest, at, w):
                for c in range(KC):
                    last = split_product(dest, wgu_hi[:, c, at:at + w], wgu_lo[:, c, at:at + w],
                                         xT_hi[:, c, :], xT_lo[:, c, :], c == 0, c == KC - 1)
                return last

            def unit(i, pair, u):
                if u == 0:
                    pe.wait_ge(xT_hi_ready, count(i, pair + 1, 1, 1))
                    pe.wait_ge(xT_lo_ready, count(i, pair + 1, 1, 1))
                need(pe, h_ready, units(i, pair, u - 1 + PAD))
                bank = unit_ps[:, u % 2, :]
                last = gate_up_chunk(bank[:, 0:TOK], 2 * u * P, P)
                if u < FULL:
                    last = gate_up_chunk(bank[:, TOK:2 * TOK], (2 * u + 1) * P, P)
                last.then_inc(unit_done, 1)

            def down(i, pair, s):
                dest = unit_ps[:, s, 0:L]
                sl = slice(s * P, (s + 1) * P)
                pe.wait_ge(h_ready, units(i, pair, NU - 1 + s + PAD))
                if s == 0:
                    pe.wait_ge(wd_hi_ready, 1)
                    pe.wait_ge(wd_lo_ready, 1)
                for u in range(NU):
                    if s == 0 and u in (0, FULL - 1, FULL):
                        done = FULL - 1 if u == 0 else u + 1
                        pe.wait_ge(h_hi_ready, units(i, pair, done))
                        if u < FULL:
                            pe.wait_ge(h_lo_ready, i * (2 * FULL) + (pair // 2 * FULL + done))
                        else:
                            pe.wait_ge(h_rest_ready, i * 2 + (pair // 2 + 1))
                    nc.tensor.matmul(dest, h_hi[:, u, sl], wd_hi[:, u, :], start=(u == 0), stop=False)
                    nc.tensor.matmul(dest, h_hi[:, u, sl], wd_lo[:, u, :], start=False, stop=False)
                    last = nc.tensor.matmul(dest, h_lo[:, u, sl], wd_hi[:, u, :], start=False, stop=(u == NU - 1))
                last.then_inc(down_done, 1)

            def keep_warm():
                for n in range(WARM):
                    nc.tensor.matmul(out_ps[:, 0:P], ident[:, :], ident[:, :], start=True, stop=True)

            def run(i, k):
                ffn = k >= 2
                pair = k - 2 - k % 2
                once = isinstance(i, int) and k < SLOTS
                convolve(i, k, 0)
                if k == 0:
                    sum_skip(0, 0)
                if k % 2 == 0:
                    turn_x(i, k - 1)
                if ffn and k % 2 == 1:
                    unit(i, pair, 4)
                convolve(i, k, 1)
                if k == 0:
                    sum_skip(0, 1)
                if once and k == 2:
                    pe.wait_ge(wgu_hi_ready, KC)
                    pe.wait_ge(wgu_lo_ready, KC)
                if ffn and k % 2 == 0:
                    unit(i, pair, 0)
                sum_heads(i, k, 0)
                turn_v(i, k + 2)
                if k < 0:
                    keep_warm()
                if k % 2 == 0:
                    if ffn:
                        unit(i, pair, 1)
                    sum_heads(i, k, 1)
                    if ffn:
                        unit(i, pair, 2)
                    if k >= 0:
                        sum_skip(i, k + 2)
                    if ffn:
                        unit(i, pair, 3)
                else:
                    if ffn:
                        unit(i, pair, 5)
                    turn_x(i, k - 1)
                    sum_heads(i, k, 1)
                    if ffn:
                        down(i, pair, 0)
                    if k >= 0:
                        sum_skip(i, k + 2)
                    if ffn:
                        down(i, pair, 1)

            run.engine = mybir.EngineType.PE
            steps(run)


def kernel(**inputs):
    import numpy as np
    import concourse.bacc as bacc
    from concourse.bass_utils import run_bass_kernel_spmd

    def tiles(a):
        return a.reshape(B, H, NH, L).transpose(1, 0, 2, 3).reshape(H, P, L)

    x, c = tiles(np.asarray(inputs["x"])), tiles(np.asarray(inputs["ctx_2048"]))
    cT = c.reshape(H, P, MB, P).transpose(0, 3, 2, 1).reshape(H, P, L)
    bias = np.broadcast_to(np.asarray(inputs["fside_S2_0"]).reshape(H, 1, NH), (H, B, NH)).reshape(H, P, 1)
    k_padded = np.concatenate([np.zeros((H, P - 1), np.float32), np.asarray(inputs["L0_xattn_k"])], axis=1)
    toeplitz = np.stack([k_padded[:, P - 1 - m:P - 1 - m + L] for m in range(P)], axis=1)
    packed = np.concatenate([x, c, cT, toeplitz, bias, np.zeros((H, P, PACK - BIAS - 1), np.float32)], axis=2).reshape(H * P, PACK)

    def columns(s, low):
        a = np.zeros((P, NU), np.float32)
        a[:, :FULL] = s[:FULL * P].reshape(FULL, P).T
        a[low:low + REST, FULL] = s[FULL * P:]
        return a

    gates = np.concatenate([np.asarray(inputs["g_xattn"]), np.asarray(inputs["g_ffn"])])
    scalars = np.concatenate([np.broadcast_to(gates, (P, 2)),
                              columns(np.asarray(inputs["L0_ffn_gate_s"]), 0),
                              columns(np.asarray(inputs["L0_ffn_up_s"]), P - REST)], axis=1)
    gw, uw = np.asarray(inputs["L0_ffn_gate_w"]), np.asarray(inputs["L0_ffn_up_w"])
    rows = []
    for u in range(NU):
        rows += [gw[u * P:(u + 1) * P], uw[u * P:(u + 1) * P]]
    gate_up = np.concatenate(rows).T.reshape(KC, P, GU).transpose(1, 0, 2)
    down = np.asarray(inputs["L0_ffn_down_w"]).T
    down_s = np.broadcast_to(np.asarray(inputs["L0_ffn_down_s"]), (P, L))

    arrays, args = {}, []
    nc = bacc.Bacc("TRN2", target_bir_lowering=False, num_devices=1)
    for name, a in (("packed", packed), ("scalars", scalars),
                    ("gate_up", gate_up), ("down", down), ("down_s", down_s)):
        arrays[name] = np.ascontiguousarray(a)
        args.append(nc.dram_tensor(name, arrays[name].shape, F32, kind="ExternalInput").ap())
    args.append(nc.dram_tensor("out", (H * P, L), F32, kind="ExternalOutput").ap())
    flamingo(nc, *args)
    r = run_bass_kernel_spmd(nc, [arrays], core_ids=[0])
    y = r.results[0]["out"]
    return y.reshape(H, B, NH, L).transpose(1, 0, 2, 3).reshape(B, D, L)
```

```python
from contextlib import ExitStack

import concourse.bass as bass
from concourse import mybir

B, D, L = 16, 128, 256
NH = 8
H = D // NH
INTER = 704
P = 128
MB = L // P
EPS = 1e-5

PAIRS = NH * B * NH
BANK = 512
KC = L // P
FULL = INTER // P
REST = INTER - FULL * P
NU = FULL + 1
GU = 2 * INTER
TOK = 2 * P
SLOTS = 4
PACK = 4 * L + 4
BIAS = 4 * L

EARLY = 2
WHOLE = 3
PAD = 2

GX, GF, GS, US = 0, 1, 2, 2 + NU
SCAL = 2 + 2 * NU

F32 = mybir.dt.float32
F32R = mybir.dt.float32r
ALU = mybir.AluOpType
ACT = mybir.ActivationFunctionType


def count(i, k, per=1, done=0):
    return i * (SLOTS * per) + (k * per + done)


def early(i, k):
    return isinstance(i, int) and SLOTS * i + k < EARLY


def whole(i, k):
    return isinstance(i, int) and SLOTS * i + k < WHOLE


def units(i, pair, done):
    return i * (2 * NU) + (pair // 2 * NU + done)


def has(i, k):
    return not isinstance(i, int) or 0 <= SLOTS * i + k < H


def need(eng, sem, value):
    if not isinstance(value, int) or value > 0:
        eng.wait_ge(sem, value)


def flamingo(nc, packed, scalars, gate_up_w, down_w, down_s, out):
    with ExitStack() as ctx:
        def sb(name, shape, dt=F32):
            return ctx.enter_context(nc.sbuf_tensor(name, shape, dt))

        def sem(name):
            return ctx.enter_context(nc.semaphore(name))

        ins = sb("ins", [P, SLOTS, PACK])
        xs = sb("xs", [P, SLOTS, L])
        x1 = sb("x1", [P, SLOTS, L])
        stats = sb("stats", [P, 2, 6])
        mv = sb("mv", [P, 2, 2])
        neg_mean = sb("neg_mean", [P, 2, 1])
        var_eps = sb("var_eps", [P, 2, 1])
        rstd = sb("rstd", [P, 2, 1])
        carrier = sb("carrier", [P, 2])
        minus_half = sb("minus_half", [P, 1])
        v = sb("v", [P, 2, L])
        vb = sb("vb", [P, 2, L])
        vbc = sb("vbc", [P, 2, L])
        skip = sb("skip", [P, 2, L])
        vT = sb("vT", [P, 2, MB * P])
        kv = sb("kv", [P, MB, PAIRS])
        kv_hi = sb("kv_hi", [P, 2, MB, PAIRS], F32R)
        kv_lo = sb("kv_lo", [P, 2, MB, PAIRS], F32R)
        T_hi = sb("T_hi", [P, 2, L], F32R)
        T_lo = sb("T_lo", [P, 2, L], F32R)
        z = sb("z", [P, MB, PAIRS])
        xn = sb("xn", [P, 2, L])
        xT_hi = sb("xT_hi", [P, KC, TOK], F32R)
        xT_lo = sb("xT_lo", [P, KC, TOK], F32R)
        gate = sb("gate", [P, 2, TOK])
        h = sb("h", [P, 2, TOK])
        h_hi = sb("h_hi", [P, NU, TOK], F32R)
        h_lo = sb("h_lo", [P, NU, TOK], F32R)
        res = sb("res", [P, 2, L])
        scal = sb("scal", [P, SCAL])
        tanh_g = sb("tanh_g", [P, 2])
        wgu = sb("wgu", [P, KC, GU])
        wgu_hi = sb("wgu_hi", [P, KC, GU], F32R)
        wgu_lo = sb("wgu_lo", [P, KC, GU], F32R)
        wd = sb("wd", [P, NU, L])
        wd_s = sb("wd_s", [P, L])
        wd_hi = sb("wd_hi", [P, NU, L], F32R)
        wd_lo = sb("wd_lo", [P, NU, L], F32R)
        ident = sb("ident", [P, P])
        same_b = sb("same_b", [P, P])

        conv = ctx.enter_context(nc.psum_tensor("conv", [P, MB, PAIRS], F32))
        unit_ps = ctx.enter_context(nc.psum_tensor("unit_ps", [P, 2, BANK], F32))
        turn_ps = ctx.enter_context(nc.psum_tensor("turn_ps", [P, BANK], F32))
        out_ps = ctx.enter_context(nc.psum_tensor("out_ps", [P, BANK], F32))

        in_loaded = [sem(f"in_loaded{s}") for s in range(SLOTS)]
        scal_loaded, wgu_loaded, wd_loaded = sem("scal_loaded"), sem("wgu_loaded"), sem("wd_loaded")
        first_x_loaded = sem("first_x_loaded")
        ident_ready, same_b_ready, const_step = sem("ident_ready"), sem("same_b_ready"), sem("const_step")
        tanh_ready, zero_ready = sem("tanh_ready"), sem("zero_ready")
        wgu_hi_ready, wgu_lo_ready = sem("wgu_hi_ready"), [sem(f"wgu_lo_ready{n}") for n in range(NU // 2)]
        wd_s_ready, wd_scaled, wd_hi_ready, wd_lo_ready = (
            sem("wd_s_ready"), sem("wd_scaled"), sem("wd_hi_ready"), sem("wd_lo_ready"))
        centered1, centered2 = sem("centered1"), sem("centered2")
        ln1_step, ln1_ready, half_ready = sem("ln1_step"), sem("ln1_ready"), sem("half_ready")
        v_ready, vb_ready, vbc_ready = sem("v_ready"), sem("vb_ready"), sem("vbc_ready")
        vT_done, vT_ready = sem("vT_done"), sem("vT_ready")
        skip_done, skip_ready, xs_ready = sem("skip_done"), sem("skip_ready"), sem("xs_ready")
        kv_ready, kv_hi_ready, kv_lo_ready = sem("kv_ready"), sem("kv_hi_ready"), sem("kv_lo_ready")
        T_hi_ready, T_lo_ready = sem("T_hi_ready"), sem("T_lo_ready")
        conv_done, z_ready, z_halved, mix_done, x1_ready = (
            sem("conv_done"), sem("z_ready"), [sem(f"z_halved{m}") for m in range(MB)], sem("mix_done"), sem("x1_ready"))
        ln2_step, ln2_ready = sem("ln2_step"), sem("ln2_ready")
        xn_ready, xT_done, xT_hi_ready, xT_lo_ready = (
            sem("xn_ready"), sem("xT_done"), sem("xT_hi_ready"), sem("xT_lo_ready"))
        unit_done, silu_ready = sem("unit_done"), sem("silu_ready")
        h_ready, h_hi_ready, h_lo_ready, h_rest_ready = (
            sem("h_ready"), sem("h_hi_ready"), sem("h_lo_ready"), sem("h_rest_ready"))
        down_done, res_ready = sem("down_done"), sem("res_ready")
        res_free = [sem(f"res_free{s}") for s in range(2)]

        def x_row(k):
            return ins[:, k % SLOTS, 0:L]

        def c_row(k):
            return ins[:, k % SLOTS, L:2 * L]

        def c_T(k, m):
            return ins[:, k % SLOTS, 2 * L + m * P:2 * L + (m + 1) * P]

        def T(k):
            return ins[:, k % SLOTS, 3 * L:4 * L]

        def bias(k):
            return ins[:, k % SLOTS, BIAS:BIAS + 1]

        def over_j(a):
            return a.rearrange("p (b i) -> p i b", i=NH).unsqueeze(3).broadcast_to([P, NH, B, NH])

        def by_ibj(a):
            return a.rearrange("p (i b j) -> p i b j", i=NH, b=B)

        def is_last(i, pair):
            return isinstance(i, int) and SLOTS * i + pair == H - 2

        def down_ps(i, pair, s):
            if is_last(i, pair):
                return conv[:, 0, 0:L] if s else out_ps[:, 0:L]
            return unit_ps[:, s, 0:L]

        def halve(eng, ops, i, k, m):
            if not has(i, k) or whole(i, k):
                return
            eng.wait_ge(z_ready, count(i, k, MB, m + 1))
            ops.tensor_tensor(z[:, m, 0:PAIRS // 2], z[:, m, 0:PAIRS // 2], z[:, m, PAIRS // 2:PAIRS],
                              ALU.add).then_inc(z_halved[m], 1)

        def gate_up_low(eng, ops, u):
            sl = slice(2 * u * P, min(2 * (u + 2) * P, GU))
            eng.wait_ge(wgu_hi_ready, KC)
            ops.tensor_tensor(wgu_lo[:, :, sl], wgu[:, :, sl], wgu_hi[:, :, sl].bitcast(F32), ALU.subtract
                              ).then_inc(wgu_lo_ready[u // 2], 1)

        def down_low(eng, ops, part):
            sl = slice(part * (NU // 2), (part + 1) * (NU // 2))
            eng.wait_ge(wd_hi_ready, 1)
            ops.tensor_tensor(wd_lo[:, sl, :], wd[:, sl, :], wd_hi[:, sl, :].bitcast(F32), ALU.subtract
                              ).then_inc(wd_lo_ready, 1)

        def steps(run):
            for k in range(-2, 2 + SLOTS):
                run(0, k)
            with nc.Fori(1, (H - 4) // SLOTS, engines=[run.engine]) as i:
                for k in range(2, 2 + SLOTS):
                    run(i, k)
            for k in range(H - 2, H + 2):
                run(0, k)

        block = ctx.enter_context(nc.Block())

        @block.sync
        def _(sp):
            def load(i, k):
                if not has(i, k):
                    return
                row = (i * SLOTS + k) * P
                need(sp, x1_ready, count(i, k - SLOTS, 1, 1))
                sp.dma_start(ins[:, k % SLOTS, :], packed[bass.ds(row, P), :]
                             ).then_inc(in_loaded[k % SLOTS], 16)

            def store(i, k):
                for s in range(2):
                    row = (i * SLOTS + k + s) * P
                    sp.wait_ge(res_ready, count(i, k + s, 1, 1))
                    sp.dma_start(out[bass.ds(row, P), :], res[:, s, :]).then_inc(res_free[s], 16)

            sp.dma_start(ins[:, 0, 0:L], packed[0:P, 0:L]).then_inc(first_x_loaded, 16)
            sp.dma_start(ins[:, 0, L:PACK], packed[0:P, L:PACK]).then_inc(in_loaded[0], 16)
            sp.dma_start(scal[:, :], scalars).then_inc(scal_loaded, 16)
            load(0, 1)
            sp.wait_ge(zero_ready, 1)
            sp.dma_start(wd[:, 0:FULL, :], down_w[0:FULL * P, :].rearrange("(c p) n -> p c n", p=P)
                         ).then_inc(wd_loaded, 16)
            sp.dma_start(wd[P - REST:P, FULL, :], down_w[FULL * P:INTER, :]).then_inc(wd_loaded, 16)
            sp.dma_start(wd_s[:, :], down_s).then_inc(wd_loaded, 16)
            load(0, 2)
            sp.dma_start(wgu[:, :, :], gate_up_w).then_inc(wgu_loaded, 16)
            load(0, 3)
            load(0, 4)
            load(0, 5)

            def turn(i, pair):
                load(i, pair + 6)
                load(i, pair + 7)
                store(i, pair)

            with nc.Fori(0, H // SLOTS - 2, engines=[mybir.EngineType.SP]) as i:
                turn(i, 0)
                turn(i, 2)
            for pair in range(H - 2 * SLOTS, H, 2):
                turn(0, pair)
            for s in range(2):
                sp.wait_ge(res_free[s], 16 * (H // 2 + 1))

        @block.gpsimd
        def _(pool):
            nc.gpsimd.memset(minus_half[:, :], -0.5).then_inc(half_ready, 1)
            nc.gpsimd.memset(ident[:, :], 0.0).then_inc(const_step, 1)
            nc.gpsimd.memset(same_b[:, :], 1.0).then_inc(const_step, 1)
            pool.wait_ge(const_step, 2)
            nc.gpsimd.affine_select(out=ident[:, :], in_=ident[:, :], compare_op=ALU.not_equal, fill=1.0, base=0,
                                    pattern=[[-1, P]], channel_multiplier=1).then_inc(ident_ready, 1)
            sb3 = same_b[:, :].rearrange("p (b j) -> p b j", j=NH)
            nc.gpsimd.affine_select(out=sb3, in_=sb3, compare_op=ALU.is_ge, fill=0.0, base=0,
                                    pattern=[[-NH, B], [0, NH]], channel_multiplier=1).then_inc(const_step, 1)
            pool.wait_ge(const_step, 3)
            nc.gpsimd.affine_select(out=sb3, in_=sb3, compare_op=ALU.is_ge, fill=0.0, base=NH - 1,
                                    pattern=[[NH, B], [0, NH]], channel_multiplier=-1).then_inc(same_b_ready, 1)

            def inverse_std(i, k, which, step, ready):
                if not has(i, k):
                    return
                if isinstance(i, int) and k == 0:
                    pool.wait_ge(half_ready, 1)
                pool.wait_ge(step, count(i, k, 4, 4))
                nc.gpsimd.tensor_tensor(rstd[:, which, :], var_eps[:, which, :], minus_half[:, :], ALU.pow
                                        ).then_inc(ready, 1)

            def products(i, k, m):
                if not has(i, k):
                    return
                if m == 0:
                    pool.wait_ge(vT_ready, count(i, k, 1, 1))
                need(pool, kv_lo_ready, count(i, k - 1, MB, m + 1))
                nc.gpsimd.tensor_tensor(by_ibj(kv[:, m, :]), over_j(vT[:, k % 2, m * P:(m + 1) * P]),
                                        c_T(k, m).rearrange("p (b j) -> p b j", j=NH).unsqueeze(1)
                                        .broadcast_to([P, NH, B, NH]), ALU.mult).then_inc(kv_ready, 1)

            def split_T(i, k):
                if not has(i, k):
                    return
                pool.wait_ge(T_hi_ready, count(i, k, 1, 1))
                nc.gpsimd.tensor_tensor(T_lo[:, k % 2, :], T(k), T_hi[:, k % 2, :].bitcast(F32),
                                        ALU.subtract).then_inc(T_lo_ready, 1)

            def skip_terms(i, k):
                if not has(i, k):
                    return
                pool.wait_ge(vb_ready, count(i, k, 1, 1))
                need(pool, skip_done, count(i, k - 2, 1, 1))
                nc.gpsimd.tensor_tensor(vbc[:, k % 2, :], vb[:, k % 2, :], c_row(k), ALU.mult
                                        ).then_inc(vbc_ready, 1)

            def add_skip(i, k):
                if not has(i, k):
                    return
                pool.wait_ge(skip_ready, count(i, k, 1, 1))
                need(pool, x1_ready, count(i, k - SLOTS, 1, 1))
                nc.gpsimd.tensor_tensor(xs[:, k % SLOTS, :], x_row(k), skip[:, k % 2, :], ALU.add
                                        ).then_inc(xs_ready, 1)

            def h_low(i, pair, u):
                pool.wait_ge(h_hi_ready, units(i, pair, u + 1))
                nc.gpsimd.tensor_tensor(h_lo[:, u, :], h[:, u % 2, :], h_hi[:, u, :].bitcast(F32),
                                        ALU.subtract).then_inc(h_lo_ready, 1)

            def run(i, k):
                ffn = k >= 2
                pair = k - 2 - k % 2
                once = isinstance(i, int) and k < SLOTS
                if k == -1 or k > 0 and k % 2 == 0:
                    products(i, k + 1, 0)
                inverse_std(i, k + 2, 0, ln1_step, ln1_ready)
                if k == -2:
                    split_T(0, 0)
                if k == -1:
                    products(0, 0, 1)
                    skip_terms(0, 0)
                    skip_terms(0, 1)
                    products(0, 1, 0)
                elif k >= 0 and k % 2 == 0:
                    if ffn:
                        halve(pool, nc.gpsimd, i, k, 0)
                    products(i, k + 1, 1)
                    if k == 0:
                        split_T(0, 1)
                        add_skip(0, 0)
                    skip_terms(i, k + 2)
                    if ffn:
                        h_low(i, pair, 0)
                    add_skip(i, k + 1)
                    if k == 0:
                        products(0, 2, 0)
                    else:
                        split_T(i, k + 1)
                    inverse_std(i, k, 1, ln2_step, ln2_ready)
                    if ffn:
                        h_low(i, pair, 1)
                        products(i, k + 2, 0)
                        h_low(i, pair, 2)
                    if once and k == 2:
                        down_low(pool, nc.gpsimd, 1)
                elif k >= 0:
                    if ffn:
                        h_low(i, pair, 3)
                    products(i, k + 1, 1)
                    if ffn:
                        h_low(i, pair, 4)
                    skip_terms(i, k + 2)
                    split_T(i, k + 1)
                    add_skip(i, k + 1)
                    if once and k == 1:
                        gate_up_low(pool, nc.gpsimd, 0)
                    inverse_std(i, k, 1, ln2_step, ln2_ready)

            run.engine = mybir.EngineType.Pool
            steps(run)

        @block.scalar
        def _(act):
            def times_bias(i, k):
                if not has(i, k):
                    return
                need(act, vbc_ready, count(i, k - 2, 1, 1))
                act.wait_ge(v_ready, count(i, k, 1, 1))
                nc.scalar.activation(vb[:, k % 2, :], v[:, k % 2, :], ACT.Copy, scale=bias(k)
                                     ).then_inc(vb_ready, 1)

            def center1(i, k):
                if not has(i, k) or early(i, k):
                    return
                act.wait_ge(ln1_step, count(i, k, 4, 4))
                need(act, vT_done, count(i, k - 2, 1, 1))
                need(act, vb_ready, count(i, k - 2, 1, 1))
                nc.scalar.activation(v[:, k % 2, :], x_row(k), ACT.Identity, bias=neg_mean[:, 0, :]
                                     ).then_inc(centered1, 1)

            def normalize1(i, k):
                if not has(i, k) or early(i, k):
                    return
                act.wait_ge(centered1, count(i, k, 1, 1 - EARLY))
                act.wait_ge(ln1_ready, count(i, k, 1, 1))
                nc.scalar.activation(v[:, k % 2, :], v[:, k % 2, :], ACT.Copy, scale=rstd[:, 0, :]
                                     ).then_inc(v_ready, 1)

            def center2(i, k):
                if not has(i, k):
                    return
                act.wait_ge(ln2_step, count(i, k, 4, 4))
                need(act, xT_done, count(i, k - 2, 1, 1))
                nc.scalar.activation(xn[:, k % 2, :], x1[:, k % SLOTS, :], ACT.Identity, bias=neg_mean[:, 1, :]
                                     ).then_inc(centered2, 1)

            def normalize2(i, k):
                if not has(i, k):
                    return
                act.wait_ge(centered2, count(i, k, 1, 1))
                act.wait_ge(ln2_ready, count(i, k, 1, 1))
                nc.scalar.activation(xn[:, k % 2, :], xn[:, k % 2, :], ACT.Copy, scale=rstd[:, 1, :]
                                     ).then_inc(xn_ready, 1)

            def copy_vT(i, k):
                if not has(i, k):
                    return
                act.wait_ge(vT_done, count(i, k, 1, 1))
                need(act, kv_ready, count(i, k - 2, MB, MB))
                nc.scalar.activation(vT[:, k % 2, :], turn_ps[:, 0:L], ACT.Copy).then_inc(vT_ready, 1)

            def kv_high(i, k, m):
                if not has(i, k):
                    return
                act.wait_ge(kv_ready, count(i, k, MB, m + 1))
                need(act, conv_done, count(i, k - 2, MB, MB))
                nc.scalar.activation(kv_hi[:, k % 2, m, :], kv[:, m, :], ACT.Copy).then_inc(kv_hi_ready, 1)

            def T_high(i, k):
                if not has(i, k):
                    return
                lap = 16 * (i + k // SLOTS + 1) if isinstance(i, int) else (i + (k // SLOTS + 1)) * 16
                act.wait_ge(in_loaded[k % SLOTS], lap)
                need(act, conv_done, count(i, k - 2, MB, MB))
                nc.scalar.activation(T_hi[:, k % 2, :], T(k), ACT.Copy).then_inc(T_hi_ready, 1)

            def xT_high(i, k):
                if not has(i, k):
                    return
                act.wait_ge(xT_done, count(i, k, 1, 1))
                nc.scalar.activation(xT_hi[:, :, (k % 2) * P:(k % 2 + 1) * P],
                                     turn_ps[:, 0:L].rearrange("p (c n) -> p c n", c=KC), ACT.Copy
                                     ).then_inc(xT_hi_ready, 1)

            def silu(i, pair, u):
                rows = REST if u == FULL else P
                lo = P - rows
                act.wait_ge(unit_done, units(i, pair, u + 1))
                need(act, h_ready, units(i, pair, u - 1 + PAD))
                nc.scalar.activation(gate[lo:P, u % 2, :], unit_ps[0:rows, u % 2, 0:TOK], ACT.Silu,
                                     scale=scal[0:rows, GS + u:GS + u + 1]).then_inc(silu_ready, 1)

            def h_high(i, pair, u):
                lo = P - REST if u == FULL else 0
                act.wait_ge(h_ready, units(i, pair, u + 1 + PAD))
                nc.scalar.activation(h_hi[lo:P, u, :], h[lo:P, u % 2, :], ACT.Copy).then_inc(h_hi_ready, 1)

            def gate_up_high(c):
                nc.scalar.activation(wgu_hi[:, c, :], wgu[:, c, :], ACT.Copy).then_inc(wgu_hi_ready, 1)

            def run(i, k):
                ffn = k >= 2
                pair = k - 2 - k % 2
                if k == -2:
                    act.wait_ge(scal_loaded, 16)
                    nc.scalar.activation(tanh_g[:, :], scal[:, GX:GF + 1], ACT.Tanh).then_inc(tanh_ready, 1)
                    T_high(0, 0)
                if k % 2 == 0:
                    xT_high(i, k - 1)
                if k not in (-1, 1):
                    T_high(i, k + 1)
                if ffn and k % 2 == 1:
                    silu(i, pair, 4)
                center1(i, k + 2)
                if k != 1:
                    kv_high(i, k + 1, 0)
                normalize1(i, k + 2)
                if k == -1:
                    act.wait_ge(wd_loaded, 3 * 16)
                    act.wait_ge(tanh_ready, 1)
                    nc.scalar.activation(wd_s[:, :], wd_s[:, :], ACT.Copy, scale=tanh_g[:, 1:2]
                                         ).then_inc(wd_s_ready, 1)
                if not ffn or k % 2 == 0:
                    times_bias(i, k + 2)
                if not ffn:
                    kv_high(i, k + 1, 1)
                    copy_vT(i, k + 2)
                if k == 0:
                    act.wait_ge(wgu_loaded, 16)
                    gate_up_high(0)
                    gate_up_high(1)
                    T_high(0, 2)
                    kv_high(0, 2, 0)
                if k == -1:
                    act.wait_ge(wd_scaled, 1)
                    nc.scalar.activation(wd_hi[:, :, :], wd[:, :, :], ACT.Copy).then_inc(wd_hi_ready, 1)
                if k == 1:
                    xT_high(0, 0)
                if ffn and k % 2 == 0:
                    silu(i, pair, 0)
                    copy_vT(i, k + 2)
                    h_high(i, pair, 0)
                    silu(i, pair, 1)
                    kv_high(i, k + 1, 1)
                    h_high(i, pair, 1)
                    silu(i, pair, 2)
                    center2(i, k)
                    h_high(i, pair, 2)
                    silu(i, pair, 3)
                    normalize2(i, k)
                    h_high(i, pair, 3)
                elif ffn:
                    h_high(i, pair, 4)
                    copy_vT(i, k + 2)
                    silu(i, pair, 5)
                    xT_high(i, k - 1)
                    times_bias(i, k + 2)
                    h_high(i, pair, 5)
                    kv_high(i, k + 1, 1)
                    center2(i, k)
                    normalize2(i, k)
                else:
                    center2(i, k)
                    normalize2(i, k)

            run.engine = mybir.EngineType.Activation
            steps(run)

        @block.vector
        def _(dve):
            nc.vector.memset(wd[:, FULL, :], 0.0).then_inc(zero_ready, 1)
            nc.vector.memset(h_hi[0:P - REST, FULL, :].bitcast(F32), 0.0).then_inc(h_ready, 1)
            for s in range(2):
                nc.vector.memset(res[:, s, :], 0.0).then_inc(res_free[s], 16)
            nc.vector.memset(h_lo[0:P - REST, FULL, :].bitcast(F32), 0.0).then_inc(h_ready, 1)

            def statistics(i, k, which, src, step):
                nc.vector.bn_stats(stats[:, which, :], src).then_inc(step, 1)
                dve.wait_ge(step, count(i, k, 4, 1))
                nc.vector.tensor_copy(carrier[:, which:which + 1], stats[:, which, 0:1]).then_inc(step, 1)
                nc.vector.bn_aggr(mv[:, which, :], stats[:, which, :]).then_inc(step, 1)
                dve.wait_ge(step, count(i, k, 4, 3))
                nc.vector.tensor_scalar(neg_mean[:, which, :], mv[:, which, 0:1], -1.0, None, ALU.mult)
                nc.vector.tensor_scalar(var_eps[:, which, :], mv[:, which, 1:2], EPS, None, ALU.add
                                        ).then_inc(step, 1)

            def early_normalize1(i, k):
                if not has(i, k) or not early(i, k):
                    return
                dve.wait_ge(ln1_ready, count(i, k, 1, 1))
                nc.vector.tensor_scalar(v[:, k % 2, :], x_row(k), mv[:, 0, 0:1], rstd[:, 0, :], ALU.subtract,
                                        ALU.mult).then_inc(v_ready, 1)

            def stats1(i, k):
                if not has(i, k):
                    return
                lap = 16 * (i + k // SLOTS + 1) if isinstance(i, int) else (i + (k // SLOTS + 1)) * 16
                if isinstance(i, int) and k == 0:
                    dve.wait_ge(first_x_loaded, 16)
                else:
                    dve.wait_ge(in_loaded[k % SLOTS], lap)
                need(dve, v_ready, count(i, k - 1, 1, 1))
                statistics(i, k, 0, x_row(k), ln1_step)

            def kv_low(i, k, m):
                if not has(i, k):
                    return
                dve.wait_ge(kv_hi_ready, count(i, k, MB, m + 1))
                nc.vector.tensor_tensor(kv_lo[:, k % 2, m, :], kv[:, m, :], kv_hi[:, k % 2, m, :].bitcast(F32),
                                        ALU.subtract).then_inc(kv_lo_ready, 1)

            def times_c(i, k, m):
                if not has(i, k):
                    return
                dve.wait_ge(conv_done, count(i, k, MB, m + 1))
                need(dve, mix_done, count(i, k - 1, 1, 1))
                nc.vector.tensor_tensor(by_ibj(z[:, m, :]), by_ibj(conv[:, m, :]), over_j(c_T(k, m)),
                                        ALU.mult).then_inc(z_ready, 1)

            def skip_product(i, k):
                if not has(i, k):
                    return
                dve.wait_ge(skip_done, count(i, k, 1, 1))
                need(dve, xs_ready, count(i, k - 2, 1, 1))
                if isinstance(i, int) and k == 0:
                    dve.wait_ge(tanh_ready, 1)
                nc.vector.scalar_tensor_tensor(out=skip[:, k % 2, :], in0=turn_ps[:, 0:L], scalar=tanh_g[:, 0:1],
                                               in1=c_row(k), op0=ALU.mult, op1=ALU.mult).then_inc(skip_ready, 1)

            def residual1(i, k):
                if not has(i, k):
                    return
                dve.wait_ge(mix_done, count(i, k, 1, 1))
                dve.wait_ge(xs_ready, count(i, k, 1, 1))
                nc.vector.scalar_tensor_tensor(out=x1[:, k % SLOTS, :], in0=out_ps[:, 0:L], scalar=tanh_g[:, 0:1],
                                               in1=xs[:, k % SLOTS, :], op0=ALU.mult, op1=ALU.add
                                               ).then_inc(x1_ready, 1)

            def stats2(i, k):
                if not has(i, k):
                    return
                dve.wait_ge(x1_ready, count(i, k, 1, 1))
                need(dve, xn_ready, count(i, k - 1, 1, 1))
                statistics(i, k, 1, x1[:, k % SLOTS, :], ln2_step)

            def xT_low(i, k):
                if not has(i, k):
                    return
                dve.wait_ge(xT_hi_ready, count(i, k, 1, 1))
                sl = slice((k % 2) * P, (k % 2 + 1) * P)
                nc.vector.tensor_tensor(xT_lo[:, :, sl], turn_ps[:, 0:L].rearrange("p (c n) -> p c n", c=KC),
                                        xT_hi[:, :, sl].bitcast(F32), ALU.subtract).then_inc(xT_lo_ready, 1)

            def times_up(i, pair, u):
                lo = P - REST if u == FULL else 0
                at = 0 if u == FULL else TOK
                dve.wait_ge(silu_ready, units(i, pair, u + 1))
                need(dve, h_lo_ready, i * (2 * FULL) + (pair // 2 * FULL + max(u - 1, 0)))
                nc.vector.scalar_tensor_tensor(out=h[lo:P, u % 2, :], in0=unit_ps[lo:P, u % 2, at:at + TOK],
                                               scalar=scal[lo:P, US + u:US + u + 1], in1=gate[lo:P, u % 2, :],
                                               op0=ALU.mult, op1=ALU.mult).then_inc(h_ready, 1)

            def h_low_rest(i, pair):
                dve.wait_ge(h_hi_ready, units(i, pair, NU))
                nc.vector.tensor_tensor(h_lo[P - REST:P, FULL, :], h[P - REST:P, FULL % 2, :],
                                        h_hi[P - REST:P, FULL, :].bitcast(F32), ALU.subtract
                                        ).then_inc(h_rest_ready, 1)

            def residual2(i, pair, s):
                tile = pair + s
                dve.wait_ge(down_done, count(i, tile, 1, 1))
                dve.wait_ge(res_free[s], (i * 2 + (pair // 2 + 1)) * 16)
                nc.vector.tensor_tensor(res[:, s, :], down_ps(i, pair, s), x1[:, tile % SLOTS, :], ALU.add
                                        ).then_inc(res_ready, 1)

            def scale_down():
                dve.wait_ge(wd_s_ready, 1)
                nc.vector.tensor_tensor(wd[:, :, :], wd[:, :, :], wd_s[:, :].unsqueeze(1)
                                        .broadcast_to([P, NU, L]), ALU.mult).then_inc(wd_scaled, 1)

            def run(i, k):
                ffn = k >= 2
                pair = k - 2 - k % 2
                once = isinstance(i, int) and k < SLOTS
                stats1(i, k + 2)
                early_normalize1(i, k + 2)
                if k == 0:
                    skip_product(0, 0)
                if k % 2 == 0:
                    xT_low(i, k - 1)
                times_c(i, k, 0)
                if k % 2 == 1:
                    halve(dve, nc.vector, i, k, 0)
                if ffn and k % 2 == 1:
                    times_up(i, pair, 4)
                if not ffn or k % 2 == 0:
                    kv_low(i, k + 1, 0)
                if k == -1:
                    scale_down()
                if k == 0:
                    skip_product(0, 1)
                times_c(i, k, 1)
                halve(dve, nc.vector, i, k, 1)
                if ffn and k % 2 == 0:
                    times_up(i, pair, 0)
                    if once and k == 2:
                        gate_up_low(dve, nc.vector, 4)
                        down_low(dve, nc.vector, 0)
                if not ffn:
                    kv_low(i, k + 1, 1)
                if k % 2 == 0:
                    if ffn:
                        times_up(i, pair, 1)
                    residual1(i, k)
                    stats2(i, k)
                    if ffn:
                        times_up(i, pair, 2)
                        kv_low(i, k + 1, 1)
                    if k >= 0:
                        skip_product(i, k + 2)
                    if ffn:
                        times_up(i, pair, 3)
                else:
                    if ffn:
                        times_up(i, pair, 5)
                    xT_low(i, k - 1)
                    if ffn:
                        h_low_rest(i, pair)
                        kv_low(i, k + 1, 0)
                    residual1(i, k)
                    stats2(i, k)
                    if ffn:
                        kv_low(i, k + 1, 1)
                    if k >= 0:
                        skip_product(i, k + 2)
                    if ffn:
                        residual2(i, pair, 0)
                        residual2(i, pair, 1)
                if k == 1:
                    gate_up_low(dve, nc.vector, 2)

            run.engine = mybir.EngineType.DVE
            steps(run)

        @block.tensor
        def _(pe):
            def split_product(dest, w_hi, w_lo, a_hi, a_lo, first, last):
                nc.tensor.matmul(dest, w_hi, a_hi, start=first, stop=False)
                nc.tensor.matmul(dest, w_hi, a_lo, start=False, stop=False)
                return nc.tensor.matmul(dest, w_lo, a_hi, start=False, stop=last)

            def convolve(i, k, lb):
                if not has(i, k):
                    return
                if lb == 0:
                    pe.wait_ge(T_lo_ready, count(i, k, 1, 1))
                pe.wait_ge(kv_lo_ready, count(i, k, MB, lb + 1))
                need(pe, z_ready, count(i, k - 1, MB, lb + 1))
                for half in range(PAIRS // BANK):
                    sl = slice(half * BANK, (half + 1) * BANK)
                    for m in range(lb + 1):
                        cols = slice((lb - m) * P, (lb - m + 1) * P)
                        last = split_product(conv[:, lb, sl], T_hi[:, k % 2, cols], T_lo[:, k % 2, cols],
                                             kv_hi[:, k % 2, m, sl], kv_lo[:, k % 2, m, sl], m == 0, m == lb)
                last.then_inc(conv_done, 1)

            def sum_heads(i, k, lb):
                if not has(i, k):
                    return
                if whole(i, k):
                    pe.wait_ge(z_ready, count(i, k, MB, lb + 1))
                else:
                    pe.wait_ge(z_halved[lb], count(i, k, 1, 1 - WHOLE))
                if lb == 0:
                    need(pe, x1_ready, count(i, k - 1, 1, 1))
                heads = NH if whole(i, k) else NH // 2
                for n in range(heads):
                    last = nc.tensor.matmul(out_ps[:, lb * P:(lb + 1) * P], z[:, lb, n * P:(n + 1) * P],
                                            ident[:, :], start=(n == 0), stop=(n == heads - 1),
                                            is_transpose=True)
                if lb == MB - 1:
                    last.then_inc(mix_done, 1)

            def turn_v(i, k):
                if not has(i, k):
                    return
                pe.wait_ge(v_ready, count(i, k, 1, 1))
                if isinstance(i, int) and k == 0:
                    pe.wait_ge(ident_ready, 1)
                if isinstance(i, int) and k == 1:
                    pe.wait_ge(vT_ready, 1)
                else:
                    need(pe, skip_ready, count(i, k - 1, 1, 1))
                if k % 2 == 0:
                    need(pe, xT_lo_ready, count(i, k - 3, 1, 1))
                for m in range(MB):
                    last = nc.tensor.transpose(turn_ps[:, m * P:(m + 1) * P], v[:, k % 2, m * P:(m + 1) * P],
                                               ident[:, :])
                last.then_inc(vT_done, 1)

            def turn_x(i, k):
                if not has(i, k):
                    return
                pe.wait_ge(xn_ready, count(i, k, 1, 1))
                if k % 2 == 1:
                    need(pe, skip_ready, min(count(i, k + 2, 1, 1), H) if isinstance(i, int)
                         else count(i, k + 2, 1, 1))
                else:
                    need(pe, vT_ready, min(count(i, k + 3, 1, 1), H) if isinstance(i, int)
                         else count(i, k + 3, 1, 1))
                for m in range(KC):
                    last = nc.tensor.transpose(turn_ps[:, m * P:(m + 1) * P], xn[:, k % 2, m * P:(m + 1) * P],
                                               ident[:, :])
                last.then_inc(xT_done, 1)

            def sum_skip(i, k):
                if not has(i, k):
                    return
                pe.wait_ge(vbc_ready, count(i, k, 1, 1))
                if isinstance(i, int) and k == 0:
                    pe.wait_ge(same_b_ready, 1)
                if isinstance(i, int) and k == 0:
                    pe.wait_ge(vT_ready, 2)
                elif isinstance(i, int) and k == 1:
                    pe.wait_ge(skip_ready, 1)
                else:
                    pe.wait_ge(vT_ready, count(i, k, 1, 1))
                if k % 2 == 1:
                    need(pe, xT_lo_ready, count(i, k - 3, 1, 1))
                nc.tensor.matmul(turn_ps[:, 0:L], same_b[:, :], vbc[:, k % 2, :], start=True, stop=True
                                 ).then_inc(skip_done, 1)

            def gate_up_chunk(dest, at, w):
                for c in range(KC):
                    last = split_product(dest, wgu_hi[:, c, at:at + w], wgu_lo[:, c, at:at + w],
                                         xT_hi[:, c, :], xT_lo[:, c, :], c == 0, c == KC - 1)
                return last

            def unit(i, pair, u):
                if u == 0:
                    pe.wait_ge(xT_lo_ready, count(i, pair + 1, 1, 1))
                if isinstance(i, int) and pair == 0 and u % 2 == 0:
                    pe.wait_ge(wgu_lo_ready[u // 2], 1)
                need(pe, h_ready, units(i, pair, u - 1 + PAD))
                bank = unit_ps[:, u % 2, :]
                last = gate_up_chunk(bank[:, 0:TOK], 2 * u * P, P)
                if u < FULL:
                    last = gate_up_chunk(bank[:, TOK:2 * TOK], (2 * u + 1) * P, P)
                last.then_inc(unit_done, 1)

            def down(i, pair, s, part=range(NU)):
                dest = down_ps(i, pair, s)
                sl = slice(s * P, (s + 1) * P)
                if 0 in part and not is_last(i, pair):
                    pe.wait_ge(h_ready, units(i, pair, NU - 1 + s + PAD))
                if s == 0 and 0 in part and isinstance(i, int) and pair == 0:
                    pe.wait_ge(wd_lo_ready, 2)
                for u in part:
                    if s == 0 and u == part[0] and u < FULL:
                        done = min(part[-1] + 1, FULL)
                        pe.wait_ge(h_lo_ready, i * (2 * FULL) + (pair // 2 * FULL + done))
                    if s == 0 and u == FULL:
                        pe.wait_ge(h_rest_ready, i * 2 + (pair // 2 + 1))
                    nc.tensor.matmul(dest, h_hi[:, u, sl], wd_hi[:, u, :], start=(u == 0), stop=False)
                    nc.tensor.matmul(dest, h_hi[:, u, sl], wd_lo[:, u, :], start=False, stop=False)
                    last = nc.tensor.matmul(dest, h_lo[:, u, sl], wd_hi[:, u, :], start=False, stop=(u == NU - 1))
                if NU - 1 in part:
                    last.then_inc(down_done, 1)

            def keep_warm(n):
                for _ in range(n):
                    nc.tensor.matmul(out_ps[:, 0:P], ident[:, :], ident[:, :], start=True, stop=True)

            def run(i, k):
                ffn = k >= 2
                pair = k - 2 - k % 2
                convolve(i, k, 0)
                if k == 0:
                    sum_skip(0, 0)
                if k % 2 == 0:
                    turn_x(i, k - 1)
                if ffn and k % 2 == 1:
                    unit(i, pair, 4)
                if k == H + 1:
                    unit(0, pair, 5)
                    for part in (range(0, 3), range(3, 4), range(4, 5), range(5, NU)):
                        for s in range(2):
                            down(0, pair, s, part)
                    return
                convolve(i, k, 1)
                if k == 0:
                    sum_skip(0, 1)
                if ffn and k % 2 == 0:
                    unit(i, pair, 0)
                sum_heads(i, k, 0)
                turn_v(i, k + 2)
                if k < 0:
                    keep_warm(8 if k == -2 else 2)
                if k % 2 == 0:
                    if ffn:
                        unit(i, pair, 1)
                    sum_heads(i, k, 1)
                    if ffn:
                        unit(i, pair, 2)
                    if k >= 0:
                        sum_skip(i, k + 2)
                    if ffn:
                        unit(i, pair, 3)
                else:
                    if ffn:
                        unit(i, pair, 5)
                    turn_x(i, k - 1)
                    if ffn:
                        down(i, pair, 0, range(FULL - 1))
                    sum_heads(i, k, 1)
                    if ffn:
                        down(i, pair, 0, range(FULL - 1, NU))
                    if k >= 0:
                        sum_skip(i, k + 2)
                    if ffn:
                        down(i, pair, 1)

            run.engine = mybir.EngineType.PE
            steps(run)


def kernel(**inputs):
    import numpy as np
    import concourse.bacc as bacc
    from concourse.bass_utils import run_bass_kernel_spmd

    def tiles(a):
        return a.reshape(B, H, NH, L).transpose(1, 0, 2, 3).reshape(H, P, L)

    x, c = tiles(np.asarray(inputs["x"])), tiles(np.asarray(inputs["ctx_2048"]))
    cT = c.reshape(H, P, MB, P).transpose(0, 3, 2, 1).reshape(H, P, L)
    bias = np.broadcast_to(np.asarray(inputs["fside_S2_0"]).reshape(H, 1, NH), (H, B, NH)).reshape(H, P, 1)
    k_padded = np.concatenate([np.zeros((H, P - 1), np.float32), np.asarray(inputs["L0_xattn_k"])], axis=1)
    toeplitz = np.stack([k_padded[:, P - 1 - m:P - 1 - m + L] for m in range(P)], axis=1)
    packed = np.concatenate([x, c, cT, toeplitz, bias, np.zeros((H, P, PACK - BIAS - 1), np.float32)], axis=2).reshape(H * P, PACK)

    def columns(s, low):
        a = np.zeros((P, NU), np.float32)
        a[:, :FULL] = s[:FULL * P].reshape(FULL, P).T
        a[low:low + REST, FULL] = s[FULL * P:]
        return a

    gates = np.concatenate([np.asarray(inputs["g_xattn"]), np.asarray(inputs["g_ffn"])])
    scalars = np.concatenate([np.broadcast_to(gates, (P, 2)),
                              columns(np.asarray(inputs["L0_ffn_gate_s"]), 0),
                              columns(np.asarray(inputs["L0_ffn_up_s"]), P - REST)], axis=1)
    gw, uw = np.asarray(inputs["L0_ffn_gate_w"]), np.asarray(inputs["L0_ffn_up_w"])
    rows = []
    for u in range(NU):
        rows += [gw[u * P:(u + 1) * P], uw[u * P:(u + 1) * P]]
    gate_up = np.concatenate(rows).T.reshape(KC, P, GU).transpose(1, 0, 2)
    down = np.asarray(inputs["L0_ffn_down_w"]).T
    down_s = np.broadcast_to(np.asarray(inputs["L0_ffn_down_s"]), (P, L))

    arrays, args = {}, []
    nc = bacc.Bacc("TRN2", target_bir_lowering=False, num_devices=1)
    for name, a in (("packed", packed), ("scalars", scalars),
                    ("gate_up", gate_up), ("down", down), ("down_s", down_s)):
        arrays[name] = np.ascontiguousarray(a)
        args.append(nc.dram_tensor(name, arrays[name].shape, F32, kind="ExternalInput").ap())
    args.append(nc.dram_tensor("out", (H * P, L), F32, kind="ExternalOutput").ap())
    flamingo(nc, *args)
    r = run_bass_kernel_spmd(nc, [arrays], core_ids=[0])
    y = r.results[0]["out"]
    return y.reshape(H, B, NH, L).transpose(1, 0, 2, 3).reshape(B, D, L)
```
